# Optimizing a Trainium2 kernel written in Bass

```python
import numpy as np
import jax
import jax.numpy as jnp

def _softmax(x, axis=-1):
    return jax.nn.softmax(x, axis=axis)

def _gelu(x):
    return jax.nn.gelu(x, approximate=True)

def _silu(x):
    return jax.nn.silu(x)

def _sigmoid(x):
    return jax.nn.sigmoid(x)

def _layernorm(x, axis=-1, eps=1e-05):
    m = jnp.mean(x, axis=axis, keepdims=True)
    v = jnp.var(x, axis=axis, keepdims=True)
    return (x - m) / jnp.sqrt(v + eps)

def _scatter_add(tgt, idx, src, axis=0):
    return tgt.at[idx].add(src)

def _segment_sum(src, seg, n):
    return jax.ops.segment_sum(src, seg, n)
kernel_name = 'mk_seq_postln_d1_jaxref_r4_8599d7'

def setup_inputs(seed: int=0):
    np.random.seed(seed)
    _w = jnp.asarray

    def _L0_attn_setup():
        import jax, jax.numpy as jnp
        import numpy as np
        import math
        E = 256
        H = 64
        B = 4
        S = 512
        key = jax.random.key(seed)
        ks = jax.random.split(key, 9)
        x = jax.random.normal(ks[0], (B, S, E), dtype=jnp.float32)

        def he(k, fan_in, shape):
            return jax.random.normal(k, shape, dtype=jnp.float32) * jnp.sqrt(2.0 / fan_in)
        wq = he(ks[1], E, (E, H))
        bq = jnp.zeros((H,), jnp.float32)
        wk = he(ks[2], E, (E, H))
        bk = jnp.zeros((H,), jnp.float32)
        wv = he(ks[3], E, (E, H))
        bv = jnp.zeros((H,), jnp.float32)
        wo = he(ks[4], H, (H, E))
        bo = jnp.zeros((E,), jnp.float32)
        return {'x': x, 'wq': wq, 'bq': bq, 'wk': wk, 'bk': bk, 'wv': wv, 'bv': bv, 'wo': wo, 'bo': bo}
    _L0_attn_in = _L0_attn_setup()

    def _L0_ffn_setup():
        import jax, jax.numpy as jnp
        import numpy as np
        DIM = 256
        DEPTH = 2
        HEADS = 8
        DIM_HEAD = 64
        WINDOW = 128
        INNER = HEADS * DIM_HEAD
        HID = int(DIM * 4 * 2 / 3)
        B, N = (2, 2048)
        QK_SCALE = 8.0

        def shift_token(t):
            t1, t2 = jnp.split(t, 2, axis=-1)
            t2 = jnp.pad(t2, ((0, 0), (1, 0), (0, 0)))[:, :-1]
            return jnp.concatenate([t1, t2], axis=-1)

        def l2norm(t):
            return t / jnp.clip(jnp.linalg.norm(t, axis=-1, keepdims=True), 1e-12)

        def rotate_half(x):
            x1, x2 = jnp.split(x, 2, axis=-1)
            return jnp.concatenate([-x2, x1], axis=-1)

        def rotary_xpos(q, k):
            n = q.shape[-2]
            half_idx = jnp.arange(0, DIM_HEAD, 2, dtype=jnp.float32)
            inv_freq = 1.0 / 10000.0 ** (half_idx / DIM_HEAD)
            t = jnp.arange(n, dtype=jnp.float32)
            freqs = t[:, None] * inv_freq[None, :]
            freqs = jnp.concatenate([freqs, freqs], axis=-1)
            base = (half_idx + 0.4 * DIM_HEAD) / (1.4 * DIM_HEAD)
            power = (t - n // 2) / float(WINDOW // 2)
            scale = base[None, :] ** power[:, None]
            scale = jnp.concatenate([scale, scale], axis=-1)
            cos, sin = (jnp.cos(freqs), jnp.sin(freqs))
            q = q * cos * scale + rotate_half(q) * sin * scale
            k = k * cos / scale + rotate_half(k) * sin / scale
            return (q, k)

        def local_attention(q, k, v):
            b, h, n, d = q.shape
            w = n // WINDOW
            bq = q.reshape(b, h, w, WINDOW, d) * QK_SCALE
            bk = k.reshape(b, h, w, WINDOW, d)
            bv = v.reshape(b, h, w, WINDOW, d)

            def look_around(t):
                p = jnp.pad(t, ((0, 0), (0, 0), (1, 0), (0, 0), (0, 0)))
                return jnp.concatenate([p[:, :, :w], p[:, :, 1:]], axis=3)
            bk, bv = (look_around(bk), look_around(bv))
            bt = jnp.arange(n).reshape(w, WINDOW)
            btp = jnp.pad(bt, ((1, 0), (0, 0)), constant_values=-1)
            btk = jnp.concatenate([btp[:w], btp[1:]], axis=1)
            sim = jnp.einsum('bhwid,bhwjd->bhwij', bq, bk)
            i = bt[:, :, None]
            j = btk[:, None, :]
            mask = (i < j) | (i > j + WINDOW) | (j == -1)
            sim = jnp.where(mask, -jnp.finfo(sim.dtype).max, sim)
            attn = jax.nn.softmax(sim, axis=-1)
            out = jnp.einsum('bhwij,bhwjd->bhwid', attn, bv)
            return out.reshape(b, h, n, d)

        def _layer(x, wqkv, qs, ksc, wo, lg, lb, w1, b1, w2, b2):
            b, n, _ = x.shape
            h = shift_token(x)
            qkv = h @ wqkv
            q, k, v = jnp.split(qkv, 3, axis=-1)
            to_heads = lambda t: t.reshape(b, n, HEADS, DIM_HEAD).transpose(0, 2, 1, 3)
            q, k, v = (to_heads(q), to_heads(k), to_heads(v))
            q = l2norm(q) * qs
            k = l2norm(k) * ksc
            q, k = rotary_xpos(q, k)
            o = local_attention(q, k, v)
            o = o.transpose(0, 2, 1, 3).reshape(b, n, INNER)
            x = x + o @ wo
            h = shift_token(x)
            mu = h.mean(-1, keepdims=True)
            var = h.var(-1, keepdims=True)
            h = (h - mu) / jnp.sqrt(var + 1e-05) * lg + lb
            h = h @ w1 + b1
            a, g = jnp.split(h, 2, axis=-1)
            h = a * jax.nn.gelu(g, approximate=False)
            x = x + h @ w2 + b2
            return x
        key = jax.random.key(seed)
        ks = jax.random.split(key, 6)
        return {'x': jax.random.normal(ks[0], (B, N, DIM), jnp.float32), 'wqkv': jax.random.normal(ks[1], (DEPTH, DIM, 3 * INNER), jnp.float32) * 0.02, 'q_scale': jnp.ones((DEPTH, DIM_HEAD), jnp.float32), 'k_scale': jnp.ones((DEPTH, DIM_HEAD), jnp.float32), 'wo': jax.random.normal(ks[2], (DEPTH, INNER, DIM), jnp.float32) * 0.02, 'ln_g': jnp.ones((DEPTH, DIM), jnp.float32), 'ln_b': jnp.zeros((DEPTH, DIM), jnp.float32), 'w1': jax.random.normal(ks[3], (DEPTH, DIM, 2 * HID), jnp.float32) * 0.02, 'b1': jnp.zeros((DEPTH, 2 * HID), jnp.float32), 'w2': jax.random.normal(ks[4], (DEPTH, HID, DIM), jnp.float32) * 0.02, 'b2': jnp.zeros((DEPTH, DIM), jnp.float32)}
    _L0_ffn_in = _L0_ffn_setup()
    _d = {'L0_attn_x': _L0_attn_in['x'], 'L0_attn_wq': _L0_attn_in['wq'], 'L0_attn_bq': _L0_attn_in['bq'], 'L0_attn_wk': _L0_attn_in['wk'], 'L0_attn_bk': _L0_attn_in['bk'], 'L0_attn_wv': _L0_attn_in['wv'], 'L0_attn_bv': _L0_attn_in['bv'], 'L0_attn_wo': _L0_attn_in['wo'], 'L0_attn_bo': _L0_attn_in['bo'], 'L0_ffn_wqkv': _L0_ffn_in['wqkv'], 'L0_ffn_q_scale': _L0_ffn_in['q_scale'], 'L0_ffn_k_scale': _L0_ffn_in['k_scale'], 'L0_ffn_wo': _L0_ffn_in['wo'], 'L0_ffn_ln_g': _L0_ffn_in['ln_g'], 'L0_ffn_ln_b': _L0_ffn_in['ln_b'], 'L0_ffn_w1': _L0_ffn_in['w1'], 'L0_ffn_b1': _L0_ffn_in['b1'], 'L0_ffn_w2': _L0_ffn_in['w2'], 'L0_ffn_b2': _L0_ffn_in['b2']}
    _x0 = _d['L0_attn_x']
    _d['L0_attn_x'] = jax.random.normal(jax.random.fold_in(jax.random.key(seed), 1), (8, 1024, 256), dtype=_x0.dtype)
    del _x0
    return _d

def reference(L0_attn_x, L0_attn_wq, L0_attn_bq, L0_attn_wk, L0_attn_bk, L0_attn_wv, L0_attn_bv, L0_attn_wo, L0_attn_bo, L0_ffn_wqkv, L0_ffn_q_scale, L0_ffn_k_scale, L0_ffn_wo, L0_ffn_ln_g, L0_ffn_ln_b, L0_ffn_w1, L0_ffn_b1, L0_ffn_w2, L0_ffn_b2):

    def _L0_attn_ref(x, wq, bq, wk, bk, wv, bv, wo, bo):
        import jax, jax.numpy as jnp
        import numpy as np
        import math
        E = 256
        H = 64
        B = 4
        S = 512
        q = x @ wq + bq
        k = x @ wk + bk
        v = x @ wv + bv
        scale = 1.0 / math.sqrt(H)
        w = jnp.einsum('bqh,bkh->bqk', q, k) * scale
        seq = x.shape[1]
        mask = jnp.triu(jnp.ones((1, seq, seq), dtype=w.dtype), 1) * -100000000000.0
        w = w + mask
        w = jax.nn.softmax(w, axis=-1)
        z = jnp.einsum('bqk,bkh->bqh', w, v)
        z = z @ wo + bo
        return z

    def _L0_ffn_ref(x, wqkv, q_scale, k_scale, wo, ln_g, ln_b, w1, b1, w2, b2):
        import jax, jax.numpy as jnp
        import numpy as np
        DIM = 256
        DEPTH = 2
        HEADS = 8
        DIM_HEAD = 64
        WINDOW = 128
        INNER = HEADS * DIM_HEAD
        HID = int(DIM * 4 * 2 / 3)
        B, N = (2, 2048)
        QK_SCALE = 8.0

        def shift_token(t):
            t1, t2 = jnp.split(t, 2, axis=-1)
            t2 = jnp.pad(t2, ((0, 0), (1, 0), (0, 0)))[:, :-1]
            return jnp.concatenate([t1, t2], axis=-1)

        def l2norm(t):
            return t / jnp.clip(jnp.linalg.norm(t, axis=-1, keepdims=True), 1e-12)

        def rotate_half(x):
            x1, x2 = jnp.split(x, 2, axis=-1)
            return jnp.concatenate([-x2, x1], axis=-1)

        def rotary_xpos(q, k):
            n = q.shape[-2]
            half_idx = jnp.arange(0, DIM_HEAD, 2, dtype=jnp.float32)
            inv_freq = 1.0 / 10000.0 ** (half_idx / DIM_HEAD)
            t = jnp.arange(n, dtype=jnp.float32)
            freqs = t[:, None] * inv_freq[None, :]
            freqs = jnp.concatenate([freqs, freqs], axis=-1)
            base = (half_idx + 0.4 * DIM_HEAD) / (1.4 * DIM_HEAD)
            power = (t - n // 2) / float(WINDOW // 2)
            scale = base[None, :] ** power[:, None]
            scale = jnp.concatenate([scale, scale], axis=-1)
            cos, sin = (jnp.cos(freqs), jnp.sin(freqs))
            q = q * cos * scale + rotate_half(q) * sin * scale
            k = k * cos / scale + rotate_half(k) * sin / scale
            return (q, k)

        def local_attention(q, k, v):
            b, h, n, d = q.shape
            w = n // WINDOW
            bq = q.reshape(b, h, w, WINDOW, d) * QK_SCALE
            bk = k.reshape(b, h, w, WINDOW, d)
            bv = v.reshape(b, h, w, WINDOW, d)

            def look_around(t):
                p = jnp.pad(t, ((0, 0), (0, 0), (1, 0), (0, 0), (0, 0)))
                return jnp.concatenate([p[:, :, :w], p[:, :, 1:]], axis=3)
            bk, bv = (look_around(bk), look_around(bv))
            bt = jnp.arange(n).reshape(w, WINDOW)
            btp = jnp.pad(bt, ((1, 0), (0, 0)), constant_values=-1)
            btk = jnp.concatenate([btp[:w], btp[1:]], axis=1)
            sim = jnp.einsum('bhwid,bhwjd->bhwij', bq, bk)
            i = bt[:, :, None]
            j = btk[:, None, :]
            mask = (i < j) | (i > j + WINDOW) | (j == -1)
            sim = jnp.where(mask, -jnp.finfo(sim.dtype).max, sim)
            attn = jax.nn.softmax(sim, axis=-1)
            out = jnp.einsum('bhwij,bhwjd->bhwid', attn, bv)
            return out.reshape(b, h, n, d)

        def _layer(x, wqkv, qs, ksc, wo, lg, lb, w1, b1, w2, b2):
            b, n, _ = x.shape
            h = shift_token(x)
            qkv = h @ wqkv
            q, k, v = jnp.split(qkv, 3, axis=-1)
            to_heads = lambda t: t.reshape(b, n, HEADS, DIM_HEAD).transpose(0, 2, 1, 3)
            q, k, v = (to_heads(q), to_heads(k), to_heads(v))
            q = l2norm(q) * qs
            k = l2norm(k) * ksc
            q, k = rotary_xpos(q, k)
            o = local_attention(q, k, v)
            o = o.transpose(0, 2, 1, 3).reshape(b, n, INNER)
            x = x + o @ wo
            h = shift_token(x)
            mu = h.mean(-1, keepdims=True)
            var = h.var(-1, keepdims=True)
            h = (h - mu) / jnp.sqrt(var + 1e-05) * lg + lb
            h = h @ w1 + b1
            a, g = jnp.split(h, 2, axis=-1)
            h = a * jax.nn.gelu(g, approximate=False)
            x = x + h @ w2 + b2
            return x
        for l in range(DEPTH):
            x = _layer(x, wqkv[l], q_scale[l], k_scale[l], wo[l], ln_g[l], ln_b[l], w1[l], b1[l], w2[l], b2[l])
        return x
    x = L0_attn_x
    x = _layernorm(x + _L0_attn_ref(x, L0_attn_wq, L0_attn_bq, L0_attn_wk, L0_attn_bk, L0_attn_wv, L0_attn_bv, L0_attn_wo, L0_attn_bo), axis=-1)
    x = _layernorm(x + _L0_ffn_ref(x, L0_ffn_wqkv, L0_ffn_q_scale, L0_ffn_k_scale, L0_ffn_wo, L0_ffn_ln_g, L0_ffn_ln_b, L0_ffn_w1, L0_ffn_b1, L0_ffn_w2, L0_ffn_b2), axis=-1)
    return x

_drawn_inputs = setup_inputs


def setup_inputs(seed=0):
    import zlib

    import numpy as np

    out = dict(_drawn_inputs(seed))
    spreads = {'L0_attn_bq': (0.0, 0.1),
     'L0_attn_bk': (0.0, 0.8),
     'L0_attn_bv': (0.0, 0.1),
     'L0_attn_bo': (0.0, 0.1),
     'L0_ffn_q_scale': (1.0, 0.6),
     'L0_ffn_k_scale': (1.0, 0.6),
     'L0_ffn_ln_g': (1.0, 0.6),
     'L0_ffn_ln_b': (0.0, 0.8),
     'L0_ffn_b1': (0.0, 0.8),
     'L0_ffn_b2': (0.0, 0.1)}
    factors = {}
    for name, (base, spread) in spreads.items():
        noise = np.random.default_rng([zlib.crc32(name.encode()), seed]).standard_normal(out[name].shape)
        drawn = base * np.exp(spread * noise) if base else spread * noise
        out[name] = jnp.asarray(drawn.astype(out[name].dtype))
    for name, factor in factors.items():
        out[name] = (out[name] * factor).astype(out[name].dtype)
    return out
```

```python
from contextlib import ExitStack

import concourse.bass as bass
from concourse import mybir

ALU = mybir.AluOpType
ACT = mybir.ActivationFunctionType
AX = mybir.AxisListType
F32 = mybir.dt.float32
F32R = mybir.dt.float32r

P = 128
B = 8
S = 1024
NW = S // P
E = 256
KE = E // P
D = 64
H = 8
INNER = H * D
DEPTH = 2
HID = E * 4 * 2 // 3
HF = HID // P
HR = HID - HF * P
W1C = 2 * HF + 1
GR = 64
EPS = 1e-5
NORM_FLOOR = 1e-24
BIG = 3e38
MASK1 = 1e11
MASK2 = 1e24

O_QKV, O_WO = 0, KE * 3 * INNER
O_W1 = O_WO + (INNER // P) * E
O_W2 = O_W1 + KE * W1C * P
NWC = O_W2 + (HF + 1) * E
WCH = DEPTH * NWC // B
TABW = NW * 4 * D
ROWS = S + 1
PB1 = W1C
NPAR = E + 2 * KE + PB1


def post_norm_block(nc, x, wqk, wv, wo0, bqk, bvo, w_all, b2, par, tab_base, tab_scale, masks, cmask, eye, zrow, out):
    x_d = nc.dram_tensor("x_rows", [(DEPTH * B) * ROWS, E], F32).ap()
    mid_d = nc.dram_tensor("mid_rows", [B * ROWS, P], F32).ap()
    wh_d = nc.dram_tensor("w_high", [P, DEPTH * NWC], F32).ap()
    wl_d = nc.dram_tensor("w_low", [P, DEPTH * NWC], F32).ap()
    tab_d = nc.dram_tensor("rope_tables", [P, DEPTH * TABW], F32).ap()
    attention_phase(nc, x, wqk, wv, wo0, bqk, bvo, w_all, tab_base, tab_scale, cmask, eye, zrow,
                    x_d, mid_d, wh_d, wl_d, tab_d)
    layers_phase(nc, b2, par, masks, eye, x_d, mid_d, wh_d, wl_d, tab_d, out)


def need(engine, semaphore, value):
    if not isinstance(value, int) or value > 0:
        engine.wait_ge(semaphore, value)


def three_pass(pe, out, lhs, rhs, start, stop):
    (lh, ll), (rh, rl) = lhs, rhs
    pe.matmul(out, lh, rh, start=start, stop=False)
    pe.matmul(out, lh, rl, start=False, stop=False)
    return pe.matmul(out, ll, rh, start=False, stop=stop)


def attention_phase(nc, x, wqk, wv, wo0, bqk, bvo, w_all, tab_base, tab_scale, cmask, eye, zrow,
                    x_d, mid_d, wh_d, wl_d, tab_d):
    with ExitStack() as ctx:
        def sb(name, shape, dt=F32):
            return ctx.enter_context(nc.sbuf_tensor(name, shape, dt))

        def ps(name, shape):
            return ctx.enter_context(nc.psum_tensor(name, shape, F32))

        def sem(name):
            return ctx.enter_context(nc.semaphore(name))

        x_nat = sb("a_x", [P, 2, NW, E])
        x_bo = sb("a_x_plus_bo", [P, NW, E])
        xT_h, xT_l = sb("a_xT_h", [P, KE, S], F32R), sb("a_xT_l", [P, KE, S], F32R)
        qT, kT = sb("a_qT", [D, S]), sb("a_kT", [D, S])
        v = sb("a_v", [P, NW, D])
        prob = sb("a_prob", [P, 2, S])
        pT = sb("a_pT", [P, 2, NW, P])
        z = sb("a_z", [P, 2, P])
        zT = sb("a_zT", [D, 2, P])
        y = sb("a_y", [P, 2, E])
        x1 = sb("a_x1", [P, 2, E])
        raw = sb("a_wraw", [P, WCH])
        raw_h, raw_l = sb("a_wraw_h", [P, WCH], F32R), sb("a_wraw_l", [P, WCH], F32R)
        wqk_s, wv_s, wo_s = sb("a_wqk", [P, KE, P]), sb("a_wv", [P, KE, D]), sb("a_wo", [D, E])
        wqk_h, wqk_l = sb("a_wqk_h", [P, KE, P], F32R), sb("a_wqk_l", [P, KE, P], F32R)
        wv_h, wv_l = sb("a_wv_h", [P, KE, D], F32R), sb("a_wv_l", [P, KE, D], F32R)
        bqk_s = sb("a_bqk", [P, 1])
        bvo_s = sb("a_bvo", [P, D + E])
        cm = sb("a_cmask", [P, S])
        ident = sb("a_ident", [P, P])
        tab = sb("a_tab", [P, NW, 4 * D])
        tsc = sb("a_tsc", [P, DEPTH, 4 * D])
        tabs = sb("a_tabs", [P, DEPTH, NW, 4 * D])
        low = sb("a_low", [P, 8])
        rsum = sb("a_rsum", [P, 8])
        rinv = sb("a_rinv", [P, 8])
        stats = sb("a_stats", [P, 8, 6])
        mv = sb("a_mv", [P, 8, 2])
        rstd = sb("a_rstd", [P, 8])
        half = sb("a_half", [P, 1])
        took = sb("a_wait_taker", [1, NW])

        score = [ps("a_scoreA", [P, S]), ps("a_scoreB", [P, S])]
        turn = [ps("a_turn0", [P, 512]), ps("a_turn1", [P, 512])]
        pz = ps("a_pz", [P, 512])
        py = ps("a_py", [P, 512])

        x_in = [sem("a_x_in0"), sem("a_x_in1")]
        consts_in, raw_in = sem("a_consts_in"), sem("a_raw_in")
        x1_out = [sem("a_x1_out0"), sem("a_x1_out1")]
        w_out, tab_out, zero_out = sem("a_w_out"), sem("a_tab_out"), sem("a_zero_out")
        s_ws, s_wsl = sem("a_wsplit_h"), sem("a_wsplit_l")
        s_half, s_tab, s_xbo = sem("a_half_set"), sem("a_tab_done"), sem("a_xbo_done")
        s_rawh, s_rawl = sem("a_raw_h_done"), sem("a_raw_l_done")
        p_xT, h_xT, l_xT = sem("a_xT_turned"), sem("a_xT_h_done"), sem("a_xT_l_done")
        p_qk, q_done, k_done = sem("a_qk_product"), sem("a_q_done"), sem("a_k_done")
        p_v, v_done = sem("a_v_product"), sem("a_v_done")
        p_s, s_low, s_exp = sem("a_score_done"), sem("a_low_done"), sem("a_exp_done")
        p_pT, pT_done = sem("a_p_turned"), sem("a_pT_done")
        s_z0, p_z, s_rinv, z_done = sem("a_z_cleared"), sem("a_z_product"), sem("a_rinv_done"), sem("a_z_done")
        p_zT, zT_done = sem("a_z_turned"), sem("a_zT_done")
        p_y, y_done = sem("a_y_product"), sem("a_y_done")
        s_mv = sem("a_mv_done")
        s_ve, s_rstd, x1_done = sem("a_vareps_done"), sem("a_rstd_done"), sem("a_x1_done")

        block = ctx.enter_context(nc.Block())
        CONSTS = 16 * (8 + DEPTH)

        def evacs(j):
            return (j + 1 + 3) // 4

        before = [sum(evacs(m) for m in range(j)) for j in range(NW + 1)]
        PER = before[NW]

        @block.sync
        def _(sp):
            sp.dma_start(ident[:], eye).then_inc(consts_in, 16)
            sp.dma_start(wqk_s[:], wqk).then_inc(consts_in, 16)
            sp.dma_start(x_nat[:, 0], x[0:S, :].rearrange("(t p) e -> p t e", p=P)).then_inc(x_in[0], 16)
            sp.dma_start(wv_s[:], wv).then_inc(consts_in, 16)
            sp.dma_start(wo_s[:], wo0).then_inc(consts_in, 16)
            sp.dma_start(bqk_s[:], bqk).then_inc(consts_in, 16)
            sp.dma_start(bvo_s[:], bvo.partition_broadcast(P)).then_inc(consts_in, 16)
            sp.dma_start(cm[:], cmask).then_inc(consts_in, 16)
            sp.dma_start(tab[:], tab_base).then_inc(consts_in, 16)
            for layer in range(DEPTH):
                sp.dma_start(tsc[:, layer], tab_scale[layer].partition_broadcast(P)).then_inc(consts_in, 16)
            sp.dma_start(x_d.rearrange("(b r) e -> b r e", r=ROWS)[:, 0, :], zrow).then_inc(zero_out, 16)
            sp.dma_start(mid_d.rearrange("(b r) e -> b r e", r=ROWS)[:, 0, :], zrow[0:B, 0:P]).then_inc(zero_out, 16)

            def batch(i, parity, more):
                b, nxt = 2 * i + parity, 1 - parity
                if more:
                    need(sp, p_xT, b * (NW // 2))
                    need(sp, s_xbo, b)
                    sp.dma_start(x_nat[:, nxt], x[bass.ds((b + 1) * S, S), :].rearrange("(t p) e -> p t e", p=P))\
                        .then_inc(x_in[nxt], 16)
                need(sp, s_rawl, b)
                sp.dma_start(raw[:], w_all[:, bass.ds(b * WCH, WCH)]).then_inc(raw_in, 16)
                for j in range(NW):
                    if j == 4:
                        sp.wait_ge(s_rawh, b + 1)
                        sp.dma_start(wh_d[:, bass.ds(b * WCH, WCH)], raw_h[:].bitcast(F32)).then_inc(w_out, 16)
                        sp.wait_ge(s_rawl, b + 1)
                        sp.dma_start(wl_d[:, bass.ds(b * WCH, WCH)], raw_l[:].bitcast(F32)).then_inc(w_out, 16)
                    sp.wait_ge(x1_done, NW * b + j + 1)
                    sp.dma_start(x_d[bass.ds(b * ROWS + 1 + j * P, P), :], x1[:, j % 2]).then_inc(x1_out[j % 2], 16)

            with sp.Fori(0, B // 2 - 1) as i:
                batch(i, 0, True)
                batch(i, 1, True)
            batch(B // 2 - 1, 0, True)
            batch(B // 2 - 1, 1, False)
            sp.wait_ge(s_tab, 1)
            sp.dma_start(tab_d, tabs[:]).then_inc(tab_out, 16)
            for j in range(2):
                sp.wait_ge(x1_out[j], 16 * B * NW // 2)
            sp.wait_ge(w_out, 32 * B)
            sp.wait_ge(tab_out, 16)
            sp.wait_ge(zero_out, 32)

        @block.gpsimd
        def _(pool):
            pool.memset(half[:], -0.5).then_inc(s_half, 1)
            pool.wait_ge(s_half, 1)
            pool.wait_ge(consts_in, CONSTS)
            for layer in range(DEPTH):
                ins = pool.tensor_tensor(tabs[:, layer], tab[:],
                                         tsc[:, layer].unsqueeze(1).to_broadcast([P, NW, 4 * D]), ALU.mult)
            ins.then_inc(s_tab, 1)
            with pool.Fori(0, B // 2) as i:
                for par_ in range(2):
                    b = 2 * i + par_
                    pool.wait_ge(x_in[par_], 16 * i + 16)
                    pool.wait_ge(y_done, NW * b)
                    pool.tensor_tensor(x_bo[:], x_nat[:, par_],
                                       bvo_s[:, D:D + E].unsqueeze(1).to_broadcast([P, NW, E]), ALU.add)\
                        .then_inc(s_xbo, 1)
                    for j in range(NW):
                        pool.wait_ge(s_ve, NW * b + j + 1)
                        pool.tensor_tensor(rstd[:, j:j + 1], mv[:, j, 1:2], half[:], ALU.pow).then_inc(s_rstd, 1)
                        if j == 1:
                            pool.wait_ge(s_rawh, b + 1)
                            pool.wait_ge(w_out, 32 * b)
                            pool.tensor_tensor(raw_l[:], raw[:], raw_h[:].bitcast(F32), ALU.subtract)\
                                .then_inc(s_rawl, 1)

        @block.scalar
        def _(act):
            act.wait_ge(consts_in, CONSTS)
            act.activation(wqk_h[:], wqk_s[:], ACT.Copy).then_inc(s_ws, 1)
            act.activation(wv_h[:], wv_s[:], ACT.Copy).then_inc(s_ws, 1)
            with act.Fori(0, B // 2) as i:
                for par_ in range(2):
                    b = 2 * i + par_
                    for n in range(NW // 2):
                        act.wait_ge(p_xT, b * (NW // 2) + n + 1)
                        if n == 0:
                            act.wait_ge(p_v, b)
                        act.activation(xT_h[:, :, n * 256:(n + 1) * 256],
                                       turn[n % 2][:].rearrange("p (k t) -> p k t", k=KE), ACT.Copy).then_inc(h_xT, 1)
                    for n in range(2):
                        act.wait_ge(q_done, 2 * b + n + 1)
                        act.activation(kT[:, n * 512:(n + 1) * 512], score[0][D:2 * D, n * 512:(n + 1) * 512],
                                       ACT.Identity, bias=bqk_s[D:2 * D, 0:1]).then_inc(k_done, 1)
                    for j in range(NW):
                        nk = j + 1
                        act.wait_ge(s_low, NW * b + j + 1)
                        act.activation(prob[:, j % 2, 0:nk * P], prob[:, j % 2, 0:nk * P], ACT.Exp,
                                       bias=low[:, j:j + 1], scale=-1.0, accum_out=rsum[:, j:j + 1]).then_inc(s_exp, 1)
                        for n in range(evacs(j)):
                            c0, c1 = 4 * n, min(4 * n + 4, nk)
                            act.wait_ge(p_pT, PER * b + before[j] + n + 1)
                            act.activation(pT[:, j % 2, c0:c1, :],
                                           turn[(before[j] + n) % 2][:, 0:(c1 - c0) * P].rearrange("p (c t) -> p c t", t=P),
                                           ACT.Copy).then_inc(pT_done, 1)
                        if j == 0:
                            act.wait_ge(raw_in, 16 * b + 16)
                            act.wait_ge(w_out, 32 * b)
                            act.activation(raw_h[:], raw[:], ACT.Copy).then_inc(s_rawh, 1)

        @block.vector
        def _(dve):
            dve.wait_ge(s_ws, 2)
            dve.wait_ge(consts_in, CONSTS)
            dve.memset(z[:], 0.0).then_inc(s_z0, 1)
            dve.wait_ge(s_z0, 1)
            dve.tensor_tensor(wqk_l[:], wqk_s[:], wqk_h[:].bitcast(F32), ALU.subtract).then_inc(s_wsl, 1)
            dve.tensor_tensor(wv_l[:], wv_s[:], wv_h[:].bitcast(F32), ALU.subtract).then_inc(s_wsl, 1)
            with dve.Fori(0, B // 2) as i:
                for par_ in range(2):
                    b = 2 * i + par_
                    for n in range(NW // 2):
                        dve.wait_ge(h_xT, b * (NW // 2) + n + 1)
                        dve.tensor_tensor(xT_l[:, :, n * 256:(n + 1) * 256],
                                          turn[n % 2][:].rearrange("p (k t) -> p k t", k=KE),
                                          xT_h[:, :, n * 256:(n + 1) * 256].bitcast(F32), ALU.subtract).then_inc(l_xT, 1)
                    for n in range(2):
                        dve.wait_ge(p_qk, 2 * b + n + 1)
                        dve.tensor_scalar(qT[:, n * 512:(n + 1) * 512], score[0][0:D, n * 512:(n + 1) * 512],
                                          bqk_s[0:D, 0:1], -float(D) ** -0.5, ALU.add, ALU.mult).then_inc(q_done, 1)
                    dve.wait_ge(p_v, b + 1)
                    dve.tensor_tensor(v[:], pz[:].rearrange("p (t d) -> p t d", d=D),
                                      bvo_s[:, 0:D].unsqueeze(1).to_broadcast([P, NW, D]), ALU.add).then_inc(v_done, 1)

                    def softmax_low(j):
                        nk = j + 1
                        dve.wait_ge(p_s, NW * b + j + 1)
                        dve.memset(took[:, j:j + 1], 0.0)
                        dve.tensor_tensor_reduce(prob[:, j % 2, 0:nk * P], score[j % 2][:, 0:nk * P],
                                                 cm[:, S - nk * P:S], 1.0, BIG, ALU.add, ALU.min,
                                                 low[:, j:j + 1]).then_inc(s_low, 1)

                    def normalise_z(j):
                        dve.wait_ge(s_exp, NW * b + j + 1)
                        dve.reciprocal(rinv[:, j:j + 1], rsum[:, j:j + 1]).then_inc(s_rinv, 1)
                        dve.wait_ge(s_rinv, NW * b + j + 1)
                        dve.wait_ge(p_z, NW * b + j + 1)
                        dve.tensor_scalar(z[:, j % 2, 0:D], pz[:, 0:D], rinv[:, j:j + 1], None, ALU.mult).then_inc(z_done, 1)

                    def turned_z(j):
                        dve.wait_ge(p_zT, NW * b + j + 1)
                        dve.tensor_copy(zT[:, j % 2], py[0:D, 0:P]).then_inc(zT_done, 1)

                    def residual_stats(j):
                        dve.wait_ge(p_y, NW * b + j + 1)
                        dve.wait_ge(s_xbo, b + 1)
                        dve.tensor_tensor(y[:, j % 2], py[:, 0:E], x_bo[:, j], ALU.add).then_inc(y_done, 1)
                        dve.wait_ge(y_done, NW * b + j + 1)
                        dve.bn_stats(stats[:, j], y[:, j % 2])
                        dve.drain()
                        dve.bn_aggr(mv[:, j], stats[:, j]).then_inc(s_mv, 1)
                        dve.wait_ge(s_mv, NW * b + j + 1)
                        dve.tensor_scalar(mv[:, j, 1:2], mv[:, j, 1:2], EPS, None, ALU.add).then_inc(s_ve, 1)

                    def layernorm(j):
                        dve.wait_ge(s_rstd, NW * b + j + 1)
                        dve.wait_ge(x1_out[j % 2], 16 * (NW // 2) * b + 16 * (j // 2))
                        dve.tensor_scalar(x1[:, j % 2], y[:, j % 2], mv[:, j, 0:1], rstd[:, j:j + 1],
                                          ALU.subtract, ALU.mult).then_inc(x1_done, 1)

                    softmax_low(0)
                    for j in range(NW):
                        if j + 1 < NW:
                            softmax_low(j + 1)
                        if j >= 1:
                            turned_z(j - 1)
                            residual_stats(j - 1)
                        normalise_z(j)
                        if j >= 1:
                            layernorm(j - 1)
                    turned_z(NW - 1)
                    residual_stats(NW - 1)
                    layernorm(NW - 1)

        @block.tensor
        def _(pe):
            pe.wait_ge(consts_in, CONSTS)
            with pe.Fori(0, B // 2) as i:
                for par_ in range(2):
                    b = 2 * i + par_
                    pe.wait_ge(x_in[par_], 16 * i + 16)
                    for n in range(NW // 2):
                        if n == 0:
                            pe.wait_ge(pT_done, PER * b)
                        if n >= 2:
                            pe.wait_ge(l_xT, b * (NW // 2) + n - 1)
                        for k in range(KE):
                            for t in range(2):
                                ins = pe.transpose(turn[n % 2][:, k * 256 + t * P:k * 256 + (t + 1) * P],
                                                   x_nat[:, par_, 2 * n + t, k * P:(k + 1) * P], ident[:])
                        ins.then_inc(p_xT, 1)
                    pe.wait_ge(s_wsl, 2)
                    for n in range(2):
                        pe.wait_ge(l_xT, b * (NW // 2) + 2 * n + 2)
                        if n == 0:
                            pe.wait_ge(s_low, NW * b)
                        c = slice(n * 512, (n + 1) * 512)
                        for k in range(KE):
                            ins = three_pass(pe, score[0][:, c], (wqk_h[:, k], wqk_l[:, k]),
                                             (xT_h[:, k, c], xT_l[:, k, c]), k == 0, k == KE - 1)
                        ins.then_inc(p_qk, 1)
                    pe.wait_ge(z_done, NW * b)
                    for t in range(NW):
                        c = slice(t * P, (t + 1) * P)
                        for k in range(KE):
                            ins = three_pass(pe, pz[:, t * D:(t + 1) * D], (xT_h[:, k, c], xT_l[:, k, c]),
                                             (wv_h[:, k], wv_l[:, k]), k == 0, k == KE - 1)
                    ins.then_inc(p_v, 1)
                    pe.wait_ge(k_done, 2 * b + 2)

                    def scores(j):
                        nk = j + 1
                        if j >= 2:
                            pe.wait_ge(s_low, NW * b + j - 1)
                        for c in range(0, nk * P, 512):
                            w = min(512, nk * P - c)
                            ins = pe.matmul(score[j % 2][:, c:c + w], qT[:, j * P:(j + 1) * P], kT[:, c:c + w],
                                            start=True, stop=True)
                        ins.then_inc(p_s, 1)

                    def turn_probs(j):
                        nk = j + 1
                        pe.wait_ge(s_exp, NW * b + j + 1)
                        for n in range(evacs(j)):
                            m = before[j] + n
                            if m >= 2:
                                pe.wait_ge(pT_done, PER * b + m - 1)
                            for c in range(4 * n, min(4 * n + 4, nk)):
                                ins = pe.transpose(turn[m % 2][:, (c - 4 * n) * P:(c - 4 * n + 1) * P],
                                                   prob[:, j % 2, c * P:(c + 1) * P], ident[:])
                            ins.then_inc(p_pT, 1)

                    def values(j):
                        pe.wait_ge(pT_done, PER * b + before[j + 1])
                        if j == 0:
                            pe.wait_ge(v_done, b + 1)
                        else:
                            pe.wait_ge(z_done, NW * b + j)
                        for c in range(j + 1):
                            ins = pe.matmul(pz[:, 0:D], pT[:, j % 2, c, :], v[:, c, :], start=c == 0, stop=c == j)
                        ins.then_inc(p_z, 1)

                    def turn_z(j):
                        pe.wait_ge(z_done, NW * b + j + 1)
                        pe.wait_ge(y_done, NW * b + j)
                        pe.transpose(py[:, 0:P], z[:, j % 2], ident[:]).then_inc(p_zT, 1)

                    def project(j):
                        pe.wait_ge(zT_done, NW * b + j + 1)
                        pe.matmul(py[:, 0:E], zT[:, j % 2], wo_s[:], start=True, stop=True).then_inc(p_y, 1)

                    scores(0)
                    for j in range(NW):
                        if j + 1 < NW:
                            scores(j + 1)
                        if j >= 1:
                            turn_z(j - 1)
                        turn_probs(j)
                        if j >= 1:
                            project(j - 1)
                        values(j)
                    turn_z(NW - 1)
                    project(NW - 1)



class Tile:

    def __init__(self, i, off, layer):
        self.i, self.off, self.layer = i, off, layer
        self.window = off % NW
        self.batch = i + off // NW
        self.first = self.window == 0

    def done(self, per, more=0):
        return per * NW * self.i + per * self.off + more

    def slot(self, ring):
        return self.off % ring

    def uses(self, ring, more=0):
        return NW // ring * self.i + self.off // ring + more

    def is_number(self, n):
        return isinstance(self.i, int) and NW * self.i + self.off == n


TILES = DEPTH * B * NW
LAYER = B * NW
LAG_MAX = 5


class Step:
    def __init__(self, i, w, layer=None):
        self.i, self.w, self.layer = i, w, layer
        self.even = w % 2 == 0

    def tile(self, lag):
        off = self.w - lag
        if isinstance(self.i, int):
            g = NW * self.i + off
            return Tile(self.i, off, g // LAYER) if 0 <= g < TILES else None
        return Tile(self.i, off, self.layer)


def all_steps(engine, step, peel_last=False):
    last = DEPTH * B - (1 if peel_last else 0)
    for w in range(NW):
        step(Step(0, w))
    with engine.Fori(1, B) as i:
        for w in range(NW):
            step(Step(i, w, 0))
    for w in range(NW):
        step(Step(B, w))
    with engine.Fori(B + 1, last) as i:
        for w in range(NW):
            step(Step(i, w, 1))
    if peel_last:
        for w in range(NW):
            step(Step(last, w))
    for w in range(LAG_MAX):
        step(Step(DEPTH * B, w))


def layers_phase(nc, b2, par, masks, eye, x_d, mid_d, wh_d, wl_d, tab_d, out):
    with ExitStack() as ctx:
        def sb(name, shape, dt=F32):
            return ctx.enter_context(nc.sbuf_tensor(name, shape, dt))

        def ps(name, shape):
            return ctx.enter_context(nc.psum_tensor(name, shape, F32))

        def sem(name):
            return ctx.enter_context(nc.semaphore(name))

        wh, wl = sb("w_h", [P, NWC], F32R), sb("w_l", [P, NWC], F32R)
        tab = sb("rope_tab", [P, NW, 4, D])
        b2_s = sb("b2_rows", [P, DEPTH, E])
        par_s = sb("columns", [P, DEPTH, 2 * KE + W1C])
        mask = sb("mask", [P, 2, 2 * P])
        ident = sb("ident", [P, P])
        half, eps = sb("minus_half", [P, 2 * H]), sb("eps", [P, 1])
        took = sb("wait_taker", [1, 4])
        x_sb = sb("x_tile", [P, 4, E + P])
        xT_h, xT_l = sb("xT_h", [P, KE, P], F32R), sb("xT_l", [P, KE, P], F32R)
        sq = sb("squares", [P, 2 * H, D])
        ss = sb("norms_sq", [P, 2 * H])
        r = sb("inv_norm", [P, 2, 2 * H])
        rt = sb("norm_clipped", [P, 2 * H])
        rope_a, rope_b = sb("rope_cos", [P, 2, H, D]), sb("rope_sin", [P, 2, H, D])
        qn, kn = sb("q_rot", [P, INNER]), sb("k_rot", [P, INNER])
        qT_h, qT_l = sb("qT_h", [P, H // 2, P], F32R), sb("qT_l", [P, H // 2, P], F32R)
        kT_h, kT_l = sb("kT_h", [P, H // 2, 2, P], F32R), sb("kT_l", [P, H // 2, 2, P], F32R)
        v = sb("v", [P, 4, INNER])
        prob = sb("prob", [P, H, 2 * P])
        least = sb("least", [P, H])
        rsum, rinv = sb("rsum", [P, H]), sb("rinv", [P, H])
        pT = sb("pT", [P, 2, 4, 2, P])
        o = sb("o", [P, INNER])
        oT_h, oT_l = sb("oT_h", [P, INNER // P, P], F32R), sb("oT_l", [P, INNER // P, P], F32R)
        mid = sb("x_mid", [P, 2, E])
        shifted = sb("x_mid_shifted", [P, 2, P])
        res = sb("residual", [P, 4, E])
        st = sb("ln_stats", [P, 2, 2, 6])
        mv = sb("ln_mean_var", [P, 2, 2])
        ve, rstd = sb("ln_var_eps", [P, 2]), sb("ln_rstd", [P, 2])
        hn = sb("h_norm", [P, 2, E])
        hv = sb("hT", [P, KE, 2 * P])
        hT_h, hT_l = sb("hT_h", [P, KE, 2 * P], F32R), sb("hT_l", [P, KE, 2 * P], F32R)
        gel, gt = sb("gelu", [P, 2, 2 * P]), sb("gated", [P, 3, 2 * P])
        gT_h, gT_l = sb("gT_h", [P, HF + 1, 2 * P], F32R), sb("gT_l", [P, HF + 1, 2 * P], F32R)
        xf = sb("x_new", [P, 2, E])
        x1 = sb("x1_tile", [P, 2, E])
        fst, fmv = sb("f_stats", [P, 2, 6]), sb("f_mean_var", [P, 2, 2])
        fve, frstd = sb("f_var_eps", [P, 2]), sb("f_rstd", [P, 2])
        fo = sb("out_tile", [P, 2, E])

        p_score = [ps("p_score0", [P, 512]), ps("p_score1", [P, 512])]
        p_turn = [ps("p_turn0", [P, 512]), ps("p_turn1", [P, 512])]
        p_wide = [ps("p_wide0", [P, 512]), ps("p_wide1", [P, 512])]
        p_val = ps("p_values", [P, 512])
        p_mix = ps("p_mixed", [P, 512])

        consts_in = sem("consts_in")
        w_in = {n: sem(f"w_{n}_in") for n in ("qkv", "wo", "w1", "w2")}
        tab_in = sem("tab_in")
        x_in = [sem(f"x_in{n}") for n in range(4)]
        x1_in = [sem(f"x1_in{n}") for n in range(2)]
        mid_out = [sem(f"mid_out{n}") for n in range(2)]
        shifted_in = [sem(f"shifted_in{n}") for n in range(2)]
        x_out = [sem(f"x_out{n}") for n in range(2)]
        out_out = [sem(f"out_out{n}") for n in range(2)]
        pe_qT, pe_kT, pe_xT, pe_oT, pe_hT = (sem(f"pe_{n}_turned") for n in ("q", "k", "x", "o", "h"))
        pe_q, pe_k, pe_v = (sem(f"pe_{n}_product") for n in ("q", "k", "v"))
        pe_s, pe_pT, pe_pv = sem("pe_scores"), sem("pe_p_turned"), sem("pe_values")
        pe_wo, pe_w1, pe_w2 = sem("pe_wo"), sem("pe_w1"), sem("pe_w2")
        act_qT, act_kT, act_xT, act_oT, act_hT = (sem(f"act_{n}T_h") for n in ("q", "k", "x", "o", "h"))
        act_sq = [sem("act_q_squares"), sem("act_k_squares")]
        act_v, act_exp, act_pT = sem("act_v"), sem("act_exp"), sem("act_pT")
        act_gelu, act_gT = sem("act_gelu"), sem("act_gT_h")
        dve_qT, dve_kT, dve_xT, dve_oT, dve_hT = (sem(f"dve_{n}T_l") for n in ("q", "k", "x", "o", "h"))
        dve_least, dve_qr, dve_kr = sem("dve_least"), sem("dve_q_rope"), sem("dve_k_rope")
        dve_ss = [sem("dve_q_norms_sq"), sem("dve_k_norms_sq")]
        dve_rt = [sem("dve_q_clip"), sem("dve_k_clip")]
        dve_rinv, dve_o, dve_mid = sem("dve_rinv"), sem("dve_o"), sem("dve_mid")
        dve_mv, dve_hn, dve_hv = sem("dve_mean_var"), sem("dve_h_norm"), sem("dve_hT")
        dve_gt, dve_gT = sem("dve_gated"), sem("dve_gT_l")
        dve_x, dve_fmv, dve_out = sem("dve_x_new"), sem("dve_f_mean_var"), sem("dve_out")
        pool_half = sem("pool_half")
        pool_ve, pool_rstd, pool_fve, pool_frstd = (sem(f"pool_{n}") for n in ("ve", "rstd", "fve", "frstd"))
        pool_r1, pool_res = sem("pool_residual_part"), sem("pool_residual")
        pool_q, pool_ka, pool_k = (sem(f"pool_{n}") for n in ("q", "k_sum", "k"))
        pool_r = [sem("pool_q_inv_norm"), sem("pool_k_inv_norm")]

        block = ctx.enter_context(nc.Block())
        CONSTS = 16 * (3 + DEPTH)

        w_at = {"qkv": (O_QKV, O_WO), "wo": (O_WO, O_W1), "w1": (O_W1, O_W2), "w2": (O_W2, NWC)}

        def weight(name, chunks):
            a, b = w_at[name]
            return tuple(t[:, a:b].rearrange("p (k n) -> p k n", k=chunks) for t in (wh, wl))

        wqkv, wo, w1, w2 = (weight("qkv", KE), weight("wo", INNER // P), weight("w1", KE), weight("w2", HF + 1))

        def blocks_of(t):
            own = t.slot(2)
            return [own] if t.first else [1 - own, own]

        def key_columns(t):
            own = t.slot(2)
            return slice(own * P, own * P + P) if t.first else slice(0, 2 * P)

        def pair_done(t, per, more=0):
            return per * (NW // 2) * t.i + per * (t.off // 2) + more

        @block.sync
        def _(sp):
            def load_weights(name, layer):
                a, b = w_at[name]
                c = layer * NWC
                sp.dma_start(wh[:, a:b].bitcast(F32), wh_d[:, c + a:c + b]).then_inc(w_in[name], 16)
                sp.dma_start(wl[:, a:b].bitcast(F32), wl_d[:, c + a:c + b]).then_inc(w_in[name], 16)

            def load_tables(layer):
                sp.dma_start(tab[:], tab_d[:, layer * TABW:(layer + 1) * TABW].rearrange(
                    "p (w c d) -> p w c d", w=NW, c=4)).then_inc(tab_in, 16)

            def load_x(t):
                row = t.batch * ROWS + 1 + t.window * P
                n = t.slot(4)
                sp.dma_start(x_sb[:, n, 0:E], x_d[bass.ds(row, P), :]).then_inc(x_in[n], 16)
                sp.dma_start(x_sb[:, n, E:E + P], x_d[bass.ds(row - 1, P), P:E]).then_inc(x_in[n], 16)

            sp.dma_start(ident[:], eye).then_inc(consts_in, 16)
            load_x(Tile(0, 0, 0))
            load_weights("qkv", 0)
            load_tables(0)
            load_x(Tile(0, 1, 0))
            sp.dma_start(mask[:], masks).then_inc(consts_in, 16)
            sp.dma_start(par_s[:], par).then_inc(consts_in, 16)
            for layer in range(DEPTH):
                sp.dma_start(b2_s[:, layer], b2[layer].partition_broadcast(P)).then_inc(consts_in, 16)
            load_weights("wo", 0)
            load_weights("w1", 0)
            load_weights("w2", 0)

            def step(st_):
                if st_.i is not None and isinstance(st_.i, int) and st_.i == B:
                    if st_.w == 0:
                        sp.wait_ge(pe_v, LAYER)
                        load_weights("qkv", 1)
                        sp.wait_ge(dve_qr, LAYER)
                        load_tables(1)
                    if st_.w == 2:
                        sp.wait_ge(pe_wo, LAYER)
                        load_weights("wo", 1)
                    if st_.w == 4:
                        sp.wait_ge(pe_w1, (HF + 1) * LAYER // 2)
                        load_weights("w1", 1)
                    if st_.w == 5:
                        sp.wait_ge(pe_w2, LAYER)
                        load_weights("w2", 1)
                t = st_.tile(1)
                if t and t.layer == 1:
                    need(sp, pool_res, t.done(1, -1))
                    row = (t.batch - B) * ROWS + 1 + t.window * P
                    sp.dma_start(x1[:, t.slot(2)], x_d[bass.ds(row, P), :]).then_inc(x1_in[t.slot(2)], 16)
                t = st_.tile(3)
                if t:
                    need(sp, mid_out[t.slot(2)], 16 * t.uses(2, 1))
                    prev = Tile(t.i, t.off - 1, t.layer)
                    need(sp, mid_out[prev.slot(2)], 16 * prev.uses(2, 1))
                    row = mid_row(t) - 1
                    sp.dma_start(shifted[:, t.slot(2)], mid_d[bass.ds(row, P), :]).then_inc(shifted_in[t.slot(2)], 16)
                t = st_.tile(5)
                if t and t.layer == 0:
                    sp.wait_ge(dve_x, t.done(1, 1))
                    row = (t.batch + B) * ROWS + 1 + t.window * P
                    sp.dma_start(x_d[bass.ds(row, P), :], xf[:, t.slot(2)]).then_inc(x_out[t.slot(2)], 16)
                t = st_.tile(2)
                if t:
                    sp.wait_ge(dve_mid, t.done(1, 1))
                    sp.dma_start(mid_d[bass.ds(mid_row(t), P), :], mid[:, t.slot(2), P:E])\
                        .then_inc(mid_out[t.slot(2)], 16)
                t = st_.tile(-2)
                if t:
                    need(sp, dve_mid, t.done(1, -3))
                    if t.layer == 1:
                        for back in (0, 1):
                            src = Tile(t.i - B, t.off - back, 0)
                            need(sp, x_out[src.slot(2)], 16 * src.uses(2, 1))
                    load_x(t)
                t = st_.tile(5)
                if t and t.layer == 1:
                    sp.wait_ge(dve_out, t.done(1, 1 - LAYER))
                    row = (t.batch - B) * S + t.window * P
                    sp.dma_start(out[bass.ds(row, P), :], fo[:, t.slot(2)]).then_inc(out_out[t.slot(2)], 16)

            def mid_row(t):
                return (t.batch - t.layer * B) * ROWS + 1 + t.window * P

            all_steps(sp, step, peel_last=True)
            for n in range(2):
                sp.wait_ge(out_out[n], 16 * LAYER // 2)
                sp.wait_ge(x_out[n], 16 * LAYER // 2)
                sp.wait_ge(mid_out[n], 16 * TILES // 2)

        @block.gpsimd
        def _(pool):
            pool.memset(half[:], -0.5)
            pool.memset(eps[:], EPS).then_inc(pool_half, 1)
            pool.wait_ge(pool_half, 1)
            pool.wait_ge(consts_in, CONSTS)

            def step(st_):
                t = st_.tile(5)
                if t and t.layer == 1:
                    n = t.slot(2)
                    pool.wait_ge(dve_fmv, t.done(1, 1 - LAYER))
                    pool.tensor_tensor(fve[:, n:n + 1], fmv[:, n, 1:2], eps[:, 0:1], ALU.add).then_inc(pool_fve, 1)
                    pool.wait_ge(pool_fve, t.done(1, 1 - LAYER))
                    pool.tensor_tensor(frstd[:, n:n + 1], fve[:, n:n + 1], half[:, 0:1], ALU.pow).then_inc(pool_frstd, 1)
                t = st_.tile(3)
                if t:
                    n = t.slot(2)
                    pool.wait_ge(dve_mv, t.done(1, 1))
                    pool.tensor_tensor(ve[:, n:n + 1], mv[:, n, 1:2], eps[:, 0:1], ALU.add).then_inc(pool_ve, 1)
                    pool.wait_ge(pool_ve, t.done(1, 1))
                    pool.tensor_tensor(rstd[:, n:n + 1], ve[:, n:n + 1], half[:, 0:1], ALU.pow).then_inc(pool_rstd, 1)
                t = st_.tile(2)
                if t:
                    pool.wait_ge(dve_mid, t.done(1, 1))
                    need(pool, dve_x, t.done(1, -3))
                    n = t.slot(4)
                    if t.layer == 0:
                        pool.tensor_tensor(res[:, n], mid[:, t.slot(2)], b2_s[:, 0], ALU.add).then_inc(pool_res, 1)
                    else:
                        pool.tensor_tensor(res[:, n], mid[:, t.slot(2)], b2_s[:, 1], ALU.add).then_inc(pool_r1, 1)
                        pool.wait_ge(x1_in[t.slot(2)], 16 * t.uses(2, 1 - LAYER // 2))
                        pool.wait_ge(pool_r1, t.done(1, 1 - LAYER))
                        pool.tensor_tensor(res[:, n], res[:, n], x1[:, t.slot(2)], ALU.add).then_inc(pool_res, 1)
                t = st_.tile(0)
                if t:
                    slot = t.slot(2)

                    def inverse_norms(n):
                        heads = slice(n * H, (n + 1) * H)
                        pool.wait_ge(dve_rt[n], t.done(1, 1))
                        pool.tensor_tensor(r[:, slot, heads], rt[:, heads], half[:, heads], ALU.pow)\
                            .then_inc(pool_r[n], 1)

                    pool.wait_ge(dve_kr, t.done(1, 1))
                    pool.tensor_tensor(rope_a[:, 1], rope_a[:, 1], rope_b[:, 1], ALU.add).then_inc(pool_ka, 1)
                    inverse_norms(1)
                    pool.wait_ge(pool_r[1], t.done(1, 1))
                    pool.wait_ge(pool_ka, t.done(1, 1))
                    need(pool, pe_kT, t.done(1))
                    pool.tensor_tensor(kn[:].rearrange("p (h d) -> p h d", h=H), rope_a[:, 1],
                                       r[:, slot, H:2 * H].unsqueeze(2).to_broadcast([P, H, D]), ALU.mult)\
                        .then_inc(pool_k, 1)
                    pool.wait_ge(dve_qr, t.done(1, 1))
                    need(pool, pe_qT, t.done(1))
                    pool.tensor_tensor(qn[:].rearrange("p (h d) -> p h d", h=H), rope_a[:, 0], rope_b[:, 0], ALU.add)\
                        .then_inc(pool_q, 1)
                    inverse_norms(0)

            all_steps(pool, step)

        @block.scalar
        def _(act):
            act.wait_ge(consts_in, CONSTS)

            def step(st_):
                t, u = st_.tile(0), st_.tile(-1)

                def turned_x(u):
                    act.wait_ge(pe_xT, u.done(1, 1))
                    act.activation(xT_h[:], p_mix[:, 0:E].rearrange("p (k t) -> p k t", k=KE), ACT.Copy).then_inc(act_xT, 1)

                if t and t.is_number(0):
                    turned_x(t)
                a = st_.tile(1)
                if a:
                    act.wait_ge(pe_qT, a.done(1, 1))
                    act.activation(qT_h[:], p_turn[0][:].rearrange("p (c t) -> p c t", t=P), ACT.Copy).then_inc(act_qT, 1)
                    act.wait_ge(pe_kT, a.done(1, 1))
                    act.activation(kT_h[:, :, a.slot(2), :], p_turn[1][:].rearrange("p (c t) -> p c t", t=P), ACT.Copy)\
                        .then_inc(act_kT, 1)
                c = st_.tile(2)
                if c:
                    act.wait_ge(pe_oT, c.done(1, 1))
                    act.activation(oT_h[:], p_val[:].rearrange("p (k t) -> p k t", t=P), ACT.Copy).then_inc(act_oT, 1)

                def probabilities(first, last):
                    cols = key_columns(a)
                    for h in range(first, last):
                        act.wait_ge(dve_least, a.done(H, h + 1))
                        act.activation(prob[:, h, cols], prob[:, h, cols], ACT.Exp, bias=least[:, h:h + 1],
                                       scale=-1.0, accum_out=rsum[:, h:h + 1]).then_inc(act_exp, 1)

                def squares(n, product):
                    act.wait_ge(product, t.done(1, 1))
                    need(act, dve_ss[n], t.done(1))
                    act.activation(sq[:, n * H:(n + 1) * H], p_wide[1 - n][:].rearrange("p (h d) -> p h d", h=H),
                                   ACT.Square).then_inc(act_sq[n], 1)

                def turned_probs(group):
                    own = blocks_of(a)
                    for n in range(2):
                        act.wait_ge(pe_pT, a.done(4, 2 * group + n + 1))
                        src = p_turn[n][:].rearrange("p (h b t) -> p h b t", h=2, b=2)
                        act.activation(pT[:, group, 2 * n:2 * n + 2, own[0] if a.first else slice(0, 2), :],
                                       src[:, :, own[0] if a.first else slice(0, 2), :], ACT.Copy).then_inc(act_pT, 1)

                if a:
                    probabilities(0, 4)
                if t:
                    squares(1, pe_k)
                if a:
                    turned_probs(0)
                    probabilities(4, 6)
                if t:
                    squares(0, pe_q)
                if a:
                    probabilities(6, 8)
                    turned_probs(1)
                f = st_.tile(4)
                if st_.even and f:
                    act.wait_ge(dve_hv, pair_done(f, 1, 1))
                    act.activation(hT_h[:], hv[:], ACT.Copy).then_inc(act_hT, 1)
                if t:
                    act.wait_ge(pe_v, t.done(1, 1))
                    act.activation(v[:, t.slot(4)], p_wide[0][:], ACT.Copy).then_inc(act_v, 1)
                if u and not (st_.even and f):
                    turned_x(u)
                if st_.even and f:
                    def gate(n):
                        act.wait_ge(pe_w1, pair_done(f, HF + 1, n + 1))
                        need(act, dve_gt, pair_done(f, HF + 1, n - 1))
                        bank = p_wide[(n + 1) % 2]
                        col = 2 * KE + HF + n
                        if n < HF:
                            act.activation(gel[:, n % 2], bank[:, 2 * P:4 * P], ACT.Gelu,
                                           bias=par_s[:, f.layer, col:col + 1]).then_inc(act_gelu, 1)
                        else:
                            act.activation(gel[0:HR, n % 2], bank[GR:GR + HR, 0:2 * P], ACT.Gelu,
                                           bias=par_s[GR:GR + HR, f.layer, col:col + 1]).then_inc(act_gelu, 1)

                    def high(n):
                        rows = P if n < HF else HR
                        act.wait_ge(dve_gt, pair_done(f, HF + 1, n + 1))
                        act.activation(gT_h[0:rows, n], gt[0:rows, n % 3], ACT.Copy).then_inc(act_gT, 1)

                    gate(0)
                    for n in range(1, HF + 1):
                        gate(n)
                        high(n - 1)
                        if u and n == 1:
                            turned_x(u)
                    high(HF)

            all_steps(act, step, peel_last=True)

        @block.vector
        def _(dve):
            dve.wait_ge(consts_in, CONSTS)

            def step(st_):
                a, t, c, g, e = (st_.tile(n) for n in (1, 0, 2, 3, 5))
                u, f = st_.tile(-1), st_.tile(4)

                def turned_x(u):
                    dve.wait_ge(act_xT, u.done(1, 1))
                    dve.tensor_tensor(xT_l[:], p_mix[:, 0:E].rearrange("p (k t) -> p k t", k=KE),
                                      xT_h[:].bitcast(F32), ALU.subtract).then_inc(dve_xT, 1)

                if t and t.is_number(0):
                    turned_x(t)
                if a:
                    dve.wait_ge(act_qT, a.done(1, 1))
                    dve.tensor_tensor(qT_l[:], p_turn[0][:].rearrange("p (c t) -> p c t", t=P),
                                      qT_h[:].bitcast(F32), ALU.subtract).then_inc(dve_qT, 1)
                    dve.wait_ge(act_kT, a.done(1, 1))
                    dve.tensor_tensor(kT_l[:, :, a.slot(2), :], p_turn[1][:].rearrange("p (c t) -> p c t", t=P),
                                      kT_h[:, :, a.slot(2), :].bitcast(F32), ALU.subtract).then_inc(dve_kT, 1)
                if c:
                    dve.wait_ge(act_oT, c.done(1, 1))
                    dve.tensor_tensor(oT_l[:], p_val[:].rearrange("p (k t) -> p k t", t=P),
                                      oT_h[:].bitcast(F32), ALU.subtract).then_inc(dve_oT, 1)
                if e:
                    n = e.slot(2)
                    dve.wait_ge(pe_w2, e.done(1, 1))
                    dve.wait_ge(pool_res, e.done(1, 1))
                    if e.layer == 0:
                        need(dve, x_out[n], 16 * e.uses(2))
                    elif e.is_number(LAYER) or e.is_number(LAYER + 1):
                        dve.wait_ge(x_out[n], 16 * LAYER // 2)
                    dve.tensor_tensor(xf[:, n], p_mix[:, 0:E], res[:, e.slot(4)], ALU.add).then_inc(dve_x, 1)
                    if e.layer == 1:
                        dve.wait_ge(dve_x, e.done(1, 1))
                        dve.bn_stats(fst[:, n], xf[:, n])
                if g:
                    n = g.slot(2)
                    dve.wait_ge(shifted_in[n], 16 * g.uses(2, 1))
                    dve.bn_stats(st[:, n, 0], mid[:, n, 0:P])
                    dve.bn_stats(st[:, n, 1], shifted[:, n])
                final = e and e.layer == 1
                if g or final:
                    dve.drain()
                if g:
                    dve.bn_aggr(mv[:, g.slot(2)], st[:, g.slot(2)]).then_inc(dve_mv, 1)
                if final:
                    dve.bn_aggr(fmv[:, e.slot(2)], fst[:, e.slot(2)]).then_inc(dve_fmv, 1)

                def least_of(group):
                    cols = key_columns(a)
                    dve.wait_ge(pe_s, a.done(2, group + 1))
                    if group == 0:
                        dve.wait_ge(pool_r[0], a.done(1, 1))
                    at = 2 * a.slot(2) + group
                    dve.memset(took[:, at:at + 1], 0.0)
                    for h in range(4 * group, 4 * group + 4):
                        c0 = h % 4 // 2 * 2 * P
                        dve.tensor_tensor_reduce(prob[:, h, cols], p_score[h % 2][:, c0 + cols.start:c0 + cols.stop],
                                                 mask[:, a.slot(2), cols], r[:, a.slot(2), h:h + 1], BIG,
                                                 ALU.add, ALU.min, least[:, h:h + 1]).then_inc(dve_least, 1)

                def rotary(n, raised, last):
                    dve.wait_ge(act_sq[n], t.done(1, 1))
                    need(dve, last, t.done(1))
                    if n == 1 and (t.is_number(0) or t.is_number(LAYER)):
                        dve.wait_ge(tab_in, 16 * (t.layer + 1))
                    bank = p_wide[1 - n]
                    src = bank[:].rearrange("p (h s d) -> p h s d", h=H, s=2)
                    table = tab[:, t.window].rearrange("p c (s d) -> p c s d", s=2)
                    dve.tensor_tensor(rope_a[:, n], bank[:].rearrange("p (h d) -> p h d", h=H),
                                      tab[:, t.window, 2 * n].unsqueeze(1).to_broadcast([P, H, D]), ALU.mult)
                    dst = rope_b[:, n].rearrange("p h (s d) -> p h s d", s=2)
                    for s in range(2):
                        ins = dve.tensor_tensor(dst[:, :, s], src[:, :, 1 - s],
                                                table[:, 2 * n + 1, s].unsqueeze(1).to_broadcast([P, H, D // 2]),
                                                ALU.mult)
                    ins.then_inc(raised, 1)

                def squared_norms(n):
                    need(dve, pool_r[n], t.done(1))
                    dve.tensor_reduce(ss[:, n * H:(n + 1) * H], sq[:, n * H:(n + 1) * H], AX.X, ALU.add)\
                        .then_inc(dve_ss[n], 1)
                    dve.wait_ge(dve_ss[n], t.done(1, 1))
                    dve.tensor_scalar(rt[:, n * H:(n + 1) * H], ss[:, n * H:(n + 1) * H], NORM_FLOOR, None, ALU.max)\
                        .then_inc(dve_rt[n], 1)

                def values(group):
                    if group == 0:
                        dve.wait_ge(act_exp, a.done(H, H))
                        dve.reciprocal(rinv[:], rsum[:]).then_inc(dve_rinv, 1)
                        dve.wait_ge(dve_rinv, a.done(1, 1))
                        need(dve, pe_oT, a.done(1))
                    dve.wait_ge(pe_pv, a.done(2, group + 1))
                    dve.tensor_tensor(o[:, group * 256:(group + 1) * 256].rearrange("p (h d) -> p h d", h=4),
                                      p_val[:, 0:256].rearrange("p (h d) -> p h d", h=4),
                                      rinv[:, 4 * group:4 * group + 4].unsqueeze(2).to_broadcast([P, 4, D]),
                                      ALU.mult).then_inc(dve_o, 1)

                if a:
                    least_of(0)
                if g:
                    n = g.slot(2)
                    dve.wait_ge(pool_rstd, g.done(1, 1))
                    need(dve, pe_hT, g.uses(2))
                    dve.tensor_scalar(hn[:, n, 0:P], mid[:, n, 0:P], mv[:, n, 0:1], rstd[:, n:n + 1],
                                      ALU.subtract, ALU.mult)
                    dve.tensor_scalar(hn[:, n, P:E], shifted[:, n], mv[:, n, 0:1], rstd[:, n:n + 1],
                                      ALU.subtract, ALU.mult).then_inc(dve_hn, 1)
                if e and e.layer == 1:
                    n = e.slot(2)
                    dve.wait_ge(pool_frstd, e.done(1, 1 - LAYER))
                    need(dve, out_out[n], 16 * e.uses(2, -LAYER // 2))
                    dve.tensor_scalar(fo[:, n], xf[:, n], fmv[:, n, 0:1], frstd[:, n:n + 1],
                                      ALU.subtract, ALU.mult).then_inc(dve_out, 1)
                if a:
                    least_of(1)
                if c:
                    n = c.slot(2)
                    dve.wait_ge(pe_wo, c.done(1, 1))
                    need(dve, mid_out[n], 16 * c.uses(2))
                    need(dve, pool_res, c.done(1, -1))
                    dve.tensor_tensor(mid[:, n], p_mix[:, 0:E], x_sb[:, c.slot(4), 0:E], ALU.add).then_inc(dve_mid, 1)
                if t:
                    rotary(1, dve_kr, pool_k)
                    squared_norms(1)
                    rotary(0, dve_qr, pool_q)
                if a:
                    values(0)
                if t:
                    squared_norms(0)
                if st_.even and f:
                    dve.wait_ge(pe_hT, pair_done(f, 1, 1))
                    for k in range(KE):
                        ins = dve.tensor_scalar(hv[:, k], p_mix[:, k * 2 * P:(k + 1) * 2 * P],
                                                par_s[:, f.layer, k:k + 1], par_s[:, f.layer, KE + k:KE + k + 1],
                                                ALU.mult, ALU.add)
                    ins.then_inc(dve_hv, 1)
                    dve.wait_ge(act_hT, pair_done(f, 1, 1))
                    dve.tensor_tensor(hT_l[:], hv[:], hT_h[:].bitcast(F32), ALU.subtract).then_inc(dve_hT, 1)
                elif u:
                    turned_x(u)
                if a:
                    values(1)
                if st_.even and f:

                    def gated(n):
                        rows = P if n < HF else HR
                        col = 2 * KE + (n if n < HF else 2 * HF)
                        dve.wait_ge(act_gelu, pair_done(f, HF + 1, n + 1))
                        need(dve, act_gT, pair_done(f, HF + 1, n - 2))
                        need(dve, dve_gT, pair_done(f, HF + 1, n - 2))
                        dve.scalar_tensor_tensor(gt[0:rows, n % 3], p_wide[(n + 1) % 2][0:rows, 0:2 * P],
                                                 par_s[0:rows, f.layer, col:col + 1], gel[0:rows, n % 2],
                                                 ALU.add, ALU.mult).then_inc(dve_gt, 1)

                    def low(n):
                        rows = P if n < HF else HR
                        dve.wait_ge(act_gT, pair_done(f, HF + 1, n + 1))
                        dve.tensor_tensor(gT_l[0:rows, n], gt[0:rows, n % 3], gT_h[0:rows, n].bitcast(F32),
                                          ALU.subtract).then_inc(dve_gT, 1)

                    gated(0)
                    for n in range(1, HF + 1):
                        gated(n)
                        low(n - 1)
                        if u and n == 1:
                            turned_x(u)
                    low(HF)

            all_steps(dve, step, peel_last=True)

        @block.tensor
        def _(pe):
            pe.wait_ge(consts_in, CONSTS)

            def step(st_):
                a, t, c, e = (st_.tile(n) for n in (1, 0, 2, 5))
                f = st_.tile(4) if st_.even else None
                u = st_.tile(-1)
                last_mid, last_pair = st_.tile(3), st_.tile(5)

                def mixed_bank_free():
                    if last_mid:
                        pe.wait_ge(dve_mid, last_mid.done(1, 1))
                    elif st_.tile(6):
                        pe.wait_ge(dve_x, st_.tile(6).done(1, 1))
                    if not st_.even and last_pair:
                        pe.wait_ge(dve_hv, pair_done(last_pair, 1, 1))

                def arrived(name, tile):
                    if tile.is_number(0) or tile.is_number(LAYER):
                        pe.wait_ge(w_in[name], 32 * (tile.layer + 1))

                def turn_qk():
                    need(pe, act_pT, a.done(4))
                    for n, (src, ready, raised) in enumerate(((qn, pool_q, pe_qT), (kn, pool_k, pe_kT))):
                        pe.wait_ge(ready, a.done(1, 1))
                        for m in range(H // 2):
                            ins = pe.transpose(p_turn[n][:, m * P:(m + 1) * P], src[:, m * P:(m + 1) * P], ident[:])
                        ins.then_inc(raised, 1)

                def scores(group):
                    if group == 0:
                        pe.wait_ge(dve_qT, a.done(1, 1))
                        pe.wait_ge(dve_kT, a.done(1, 1))
                        need(pe, dve_least, a.done(H))
                    else:
                        pe.wait_ge(dve_least, a.done(H, 4))
                    cols = key_columns(a)
                    for h in range(4 * group, 4 * group + 4):
                        rows, m, c0 = slice(h % 2 * D, (h % 2 + 1) * D), h // 2, h % 4 // 2 * 2 * P
                        kh, kl = (x_[rows, m].rearrange("p b t -> p (b t)")[:, cols] for x_ in (kT_h, kT_l))
                        ins = three_pass(pe, p_score[h % 2][:, c0 + cols.start:c0 + cols.stop],
                                         (qT_h[rows, m], qT_l[rows, m]), (kh, kl), True, True)
                    ins.then_inc(pe_s, 1)

                def turn_probs(group):
                    for n in range(2):
                        pe.wait_ge(act_exp, a.done(H, 4 * group + 2 * n + 2))
                        if group == 1:
                            pe.wait_ge(act_pT, a.done(4, n + 1))
                        for hh in range(2):
                            h = 4 * group + 2 * n + hh
                            for b in blocks_of(a):
                                ins = pe.transpose(p_turn[n][:, (2 * hh + b) * P:(2 * hh + b + 1) * P],
                                                   prob[:, h, b * P:(b + 1) * P], ident[:])
                        ins.then_inc(pe_pT, 1)

                def values(group):
                    if group == 0:
                        pe.wait_ge(act_v, a.done(1, 1))
                        if c:
                            pe.wait_ge(dve_oT, c.done(1, 1))
                    else:
                        pe.wait_ge(dve_o, a.done(2, 1))
                    pe.wait_ge(act_pT, a.done(4, 2 * group + 2))
                    blocks = blocks_of(a)
                    for hh in range(4):
                        h = 4 * group + hh
                        for b in blocks:
                            slot = a.slot(4) if b == a.slot(2) else (a.off - 1) % 4
                            ins = pe.matmul(p_val[:, hh * D:(hh + 1) * D], pT[:, group, hh, b],
                                            v[:, slot, h * D:(h + 1) * D], start=b == blocks[0], stop=b == blocks[-1])
                    ins.then_inc(pe_pv, 1)

                def project(n, bank, raised):
                    for k in range(KE):
                        cols = slice(n * INNER, (n + 1) * INNER)
                        ins = three_pass(pe, bank[:], (xT_h[:, k], xT_l[:, k]), (wqkv[0][:, k, cols], wqkv[1][:, k, cols]),
                                         k == 0, k == KE - 1)
                    ins.then_inc(raised, 1)

                def turn_x(u):
                    n = u.slot(4)
                    pe.wait_ge(x_in[n], 32 * u.uses(4, 1))
                    for k in range(KE):
                        ins = pe.transpose(p_mix[:, k * P:(k + 1) * P], x_sb[:, n, k * E:k * E + P], ident[:])
                    ins.then_inc(pe_xT, 1)

                if t and t.is_number(0):
                    turn_x(t)
                if a:
                    turn_qk()
                if c:
                    pe.wait_ge(dve_o, c.done(2, 2))
                    for m in range(INNER // P):
                        ins = pe.transpose(p_val[:, m * P:(m + 1) * P], o[:, m * P:(m + 1) * P], ident[:])
                    ins.then_inc(pe_oT, 1)
                if e:
                    if t:
                        pe.wait_ge(dve_xT, t.done(1, 1))
                    else:
                        mixed_bank_free()
                    arrived("w2", e)
                    pair = Tile(e.i, e.off - e.slot(2), e.layer)
                    pe.wait_ge(dve_gT, pair_done(pair, HF + 1, HF))
                    c0 = e.slot(2) * P
                    for n in range(HF + 1):
                        rows = P if n < HF else HR
                        if n == HF:
                            pe.wait_ge(dve_gT, pair_done(pair, HF + 1, HF + 1))
                        ins = three_pass(pe, p_mix[:, 0:E], (gT_h[0:rows, n, c0:c0 + P], gT_l[0:rows, n, c0:c0 + P]),
                                         (w2[0][0:rows, n], w2[1][0:rows, n]), n == 0, n == HF)
                    ins.then_inc(pe_w2, 1)
                if a:
                    scores(0)
                if t:
                    if not e:
                        pe.wait_ge(dve_xT, t.done(1, 1))
                    need(pe, act_v, t.done(1))
                    if not st_.even and last_pair:
                        pe.wait_ge(dve_gt, pair_done(last_pair, HF + 1, HF + 1))
                    arrived("qkv", t)
                    project(1, p_wide[0], pe_k)
                if c:
                    if e:
                        pe.wait_ge(dve_x, e.done(1, 1))
                    pe.wait_ge(dve_oT, c.done(1, 1))
                    arrived("wo", c)
                    for m in range(INNER // P):
                        ins = three_pass(pe, p_mix[:, 0:E], (oT_h[:, m], oT_l[:, m]), (wo[0][:, m], wo[1][:, m]),
                                         m == 0, m == INNER // P - 1)
                    ins.then_inc(pe_wo, 1)
                if a:
                    scores(1)
                    turn_probs(0)
                if t:
                    need(pe, dve_qr, t.done(1))
                    project(0, p_wide[1], pe_q)
                if f:
                    if c:
                        pe.wait_ge(dve_mid, c.done(1, 1))
                    elif e:
                        pe.wait_ge(dve_x, e.done(1, 1))
                    pe.wait_ge(dve_hn, f.done(1, 2))
                    for k in range(KE):
                        for m in range(2):
                            ins = pe.transpose(p_mix[:, (2 * k + m) * P:(2 * k + m + 1) * P],
                                               hn[:, m, k * P:(k + 1) * P], ident[:])
                    ins.then_inc(pe_hT, 1)
                if a:
                    values(0)
                    turn_probs(1)
                if t:
                    pe.wait_ge(dve_kr, t.done(1, 1))
                    project(2, p_wide[0], pe_v)
                if u and not f:
                    if c:
                        pe.wait_ge(dve_mid, c.done(1, 1))
                    elif t:
                        pe.wait_ge(dve_xT, t.done(1, 1))
                    turn_x(u)
                if a:
                    values(1)
                if f:
                    pe.wait_ge(dve_hT, pair_done(f, 1, 1))
                    arrived("w1", f)
                    for n in range(HF + 1):
                        if n == 0 and t:
                            pe.wait_ge(dve_qr, t.done(1, 1))
                        elif n == 1 and t:
                            pe.wait_ge(act_v, t.done(1, 1))
                        elif n >= 2:
                            pe.wait_ge(dve_gt, pair_done(f, HF + 1, n - 1))
                        bank = p_wide[(n + 1) % 2]
                        parts = [(n, 0, P), (HF + n, 2 * P, P)] if n < HF else [(2 * HF, 0, GR + HR)]
                        for chunk, at, width in parts:
                            for k in range(KE):
                                cols = slice(chunk * P, chunk * P + width)
                                ins = three_pass(pe, bank[0:width, at:at + 2 * P],
                                                 (w1[0][:, k, cols], w1[1][:, k, cols]), (hT_h[:, k], hT_l[:, k]),
                                                 k == 0, k == KE - 1)
                        ins.then_inc(pe_w1, 1)
                        if u and n == 1:
                            pe.wait_ge(dve_hv, pair_done(f, 1, 1))
                            turn_x(u)

            all_steps(pe, step, peel_last=True)


def kernel(**inputs):
    import numpy as np
    import concourse.bacc as bacc
    from concourse.bass_utils import run_bass_kernel_spmd

    a = {n.removeprefix("L0_"): np.asarray(v) for n, v in inputs.items()}

    def chunks(w, width=None):
        rows = -(-w.shape[0] // P) * P
        full = np.zeros((rows, w.shape[1]), w.dtype)
        full[:w.shape[0]] = w
        return full.reshape(rows // P, P, w.shape[1]).transpose(1, 0, 2)

    def by_chunk(w):
        tail = np.zeros(w.shape[:-1] + (P,), w.dtype)
        tail[..., 0:HR] = w[..., HF * P:HID]
        tail[..., GR:GR + HR] = w[..., HID + HF * P:]
        return np.concatenate([w[..., 0:HF * P], w[..., HID:HID + HF * P], tail], axis=-1)

    w_all = np.concatenate([
        np.concatenate([chunks(w).reshape(P, -1) for w in (
            a["ffn_wqkv"][n], a["ffn_wo"][n], by_chunk(a["ffn_w1"][n]), a["ffn_w2"][n])], axis=1)
        for n in range(DEPTH)], axis=1)
    par = np.stack([np.concatenate([
        a["ffn_ln_g"][n].reshape(KE, P).T, a["ffn_ln_b"][n].reshape(KE, P).T,
        by_chunk(a["ffn_b1"][n]).reshape(W1C, P).T], axis=1) for n in range(DEPTH)], axis=1)
    swap = lambda s: np.concatenate([s[..., D // 2:], s[..., :D // 2]], axis=-1)
    qs, ks = a["ffn_q_scale"], a["ffn_k_scale"]
    tab_scale = np.concatenate([qs, swap(qs), ks, swap(ks)], axis=-1)

    f = np.float32
    half_idx = np.arange(0, D, 2, dtype=f)
    inv_freq = (f(1) / np.power(f(10000), half_idx / f(D))).astype(f)
    pos = np.arange(S, dtype=f)
    angle = np.tile((pos[:, None] * inv_freq[None, :]).astype(f), (1, 2)).astype(np.float64)
    base = ((half_idx + f(0.4 * D)) / f(1.4 * D)).astype(f).astype(np.float64)
    power = ((pos - S // 2) / f(P // 2)).astype(np.float64)
    decay = np.tile(base[None, :] ** power[:, None], (1, 2))
    sign = np.where(np.arange(D) < D // 2, -1.0, 1.0)
    tab_base = np.concatenate([-8 * np.cos(angle) * decay, -8 * sign * np.sin(angle) * decay,
                               np.cos(angle) / decay, sign * np.sin(angle) / decay], axis=1)
    tab_base = tab_base.astype(f).reshape(NW, P, 4 * D).transpose(1, 0, 2)
    i, j = np.arange(P)[:, None], np.arange(P)[None, :]
    own, prev = np.where(j > i, f(MASK2), f(0)), np.where(j < i, f(MASK2), f(0))
    masks = np.stack([np.concatenate([own, prev], 1), np.concatenate([prev, own], 1)], axis=1)
    cmask = np.zeros((P, S), f)
    cmask[:, S - P:] = np.where(j > i, f(MASK1), f(0))

    arrays = {
        "x": a["attn_x"].reshape(B * S, E),
        "wqk": chunks(np.concatenate([a["attn_wq"], a["attn_wk"]], axis=1)),
        "wv": chunks(a["attn_wv"]),
        "wo0": a["attn_wo"],
        "bqk": np.concatenate([a["attn_bq"], a["attn_bk"]])[:, None],
        "bvo": np.concatenate([a["attn_bv"], a["attn_bo"]]),
        "w_all": w_all,
        "b2": a["ffn_b2"],
        "par": par,
        "tab_base": tab_base,
        "tab_scale": tab_scale,
        "masks": masks,
        "cmask": cmask,
        "eye": np.eye(P, dtype=f),
        "zrow": np.zeros((DEPTH * B, E), f),
    }
    nc = bacc.Bacc("TRN2", target_bir_lowering=False, num_devices=1)
    arrays = {f"in_{n}": np.ascontiguousarray(v) for n, v in arrays.items()}
    t = {n[3:]: nc.dram_tensor(n, v.shape, F32, kind="ExternalInput").ap() for n, v in arrays.items()}
    out = nc.dram_tensor("out_rows", (B * S, E), F32, kind="ExternalOutput").ap()
    post_norm_block(nc, out=out, **t)
    got = run_bass_kernel_spmd(nc, [arrays], core_ids=[0])
    return got.results[0]["out_rows"].reshape(B, S, E)
```

```python
from contextlib import ExitStack

import concourse.bass as bass
from concourse import mybir

ALU = mybir.AluOpType
ACT = mybir.ActivationFunctionType
AX = mybir.AxisListType
F32 = mybir.dt.float32
F32R = mybir.dt.float32r

P = 128
B = 8
S = 1024
NW = S // P
E = 256
KE = E // P
D = 64
H = 8
INNER = H * D
DEPTH = 2
HID = E * 4 * 2 // 3
HF = HID // P
HR = HID - HF * P
W1C = 2 * HF + 1
GR = 64
EPS = 1e-5
NORM_FLOOR = 1e-24
BIG = 3e38
MASK1 = 1e11
MASK2 = 1e24

O_QKV, O_WO = 0, KE * 3 * INNER
O_W1 = O_WO + (INNER // P) * E
O_W2 = O_W1 + KE * W1C * P
NWC = O_W2 + (HF + 1) * E
WCH = DEPTH * NWC // B
WPART = WCH // 4
QKV_PARTS = 8
TABW = NW * 4 * D
ROWS = S + 1
PB1 = W1C
NPAR = E + 2 * KE + PB1


def post_norm_block(nc, x, wqk, wv, wo0, bqk, bvo, w_all, b2, par, tab_base, tab_scale, masks, cmask, eye, zrow, out):
    x_d = nc.dram_tensor("x_rows", [(DEPTH * B) * ROWS, E], F32).ap()
    mid_d = nc.dram_tensor("mid_rows", [B * ROWS, P], F32).ap()
    wh_d = nc.dram_tensor("w_high", [P, DEPTH * NWC], F32).ap()
    wl_d = nc.dram_tensor("w_low", [P, DEPTH * NWC], F32).ap()
    tab_d = nc.dram_tensor("rope_tables", [P, TABW], F32).ap()
    with ExitStack() as ctx:
        def sb(name, shape, dt=F32):
            return ctx.enter_context(nc.sbuf_tensor(name, shape, dt))

        shared = dict(
            ident=sb("ident", [P, P]), mask=sb("mask", [P, 2, 2 * P]), b2_s=sb("b2_rows", [P, DEPTH, E]),
            par_s=sb("columns", [P, DEPTH, 2 * KE + W1C]), rope=sb("rope_tab", [P, NW, 4, D]),
            wq_h=sb("wqkv_h", [P, O_WO], F32R), wq_l=sb("wqkv_l", [P, O_WO], F32R))
        attention_phase(nc, x, wqk, wv, wo0, bqk, bvo, w_all, b2, par, tab_base, tab_scale, masks, cmask, eye, zrow,
                        x_d, mid_d, wh_d, wl_d, tab_d, shared)
        layers_phase(nc, x_d, mid_d, wh_d, wl_d, tab_d, out, shared)


def need(engine, semaphore, value):
    if not isinstance(value, int) or value > 0:
        engine.wait_ge(semaphore, value)


def three_pass(pe, out, lhs, rhs, start, stop):
    (lh, ll), (rh, rl) = lhs, rhs
    pe.matmul(out, lh, rh, start=start, stop=False)
    pe.matmul(out, lh, rl, start=False, stop=False)
    return pe.matmul(out, ll, rh, start=False, stop=stop)


def attention_phase(nc, x, wqk, wv, wo0, bqk, bvo, w_all, b2, par, tab_base, tab_scale, masks, cmask, eye, zrow,
                    x_d, mid_d, wh_d, wl_d, tab_d, shared):
    with ExitStack() as ctx:
        def sb(name, shape, dt=F32):
            return ctx.enter_context(nc.sbuf_tensor(name, shape, dt))

        def ps(name, shape):
            return ctx.enter_context(nc.psum_tensor(name, shape, F32))

        def sem(name):
            return ctx.enter_context(nc.semaphore(name))

        x_nat = sb("a_x", [P, 2, NW, E])
        x_bo = sb("a_x_plus_bo", [P, 4, E])
        xT = sb("a_xT", [P, KE, S])
        qf, kf = sb("a_q", [D, S // 2]), sb("a_k", [D, S // 2])
        qT_h, qT_l = sb("a_qT_h", [D, 2, S], F32R), sb("a_qT_l", [D, 2, S], F32R)
        kT_h, kT_l = sb("a_kT_h", [D, 2, S], F32R), sb("a_kT_l", [D, 2, S], F32R)
        v = sb("a_v", [P, 2, NW, D])
        prob = sb("a_prob", [P, 4, S])
        pT = sb("a_pT", [P, 2, NW, P])
        z = sb("a_z", [P, 2, P])
        zT = sb("a_zT", [D, 2, P])
        y = sb("a_y", [P, 2, E])
        x1 = sb("a_x1", [P, 2, E])
        raw = sb("a_wraw", [P, WCH])
        raw_h, raw_l = sb("a_wraw_h", [P, WCH], F32R), sb("a_wraw_l", [P, WCH], F32R)
        wqk_s, wv_s, wo_s = sb("a_wqk", [P, KE, P]), sb("a_wv", [P, KE, D]), sb("a_wo", [D, E])
        bqk_s = sb("a_bqk", [P, 1])
        bvo_s = sb("a_bvo", [P, D + E])
        cm = sb("a_cmask", [P, S])
        ident, rope = shared["ident"], shared["rope"]
        tab = sb("a_tab", [P, NW, 4 * D])
        tsc = sb("a_tsc", [P, DEPTH, 4 * D])
        tab1 = sb("a_tab_layer1", [P, NW, 4 * D])
        low = sb("a_low", [P, NW])
        rsum, rinv = sb("a_rsum", [P, NW]), sb("a_rinv", [P, NW])
        stats = sb("a_stats", [P, NW, 6])
        mv = sb("a_mv", [P, NW, 2])
        rstd = sb("a_rstd", [P, NW])
        half = sb("a_half", [P, 1])
        took = sb("a_wait_taker", [1, NW])

        score = [ps("a_scoreA", [P, S]), ps("a_scoreB", [P, S])]
        turn = [ps("a_turn0", [P, 512]), ps("a_turn1", [P, 512])]
        pz = ps("a_pz", [P, 512])
        py = ps("a_py", [P, 512])

        x0_in = [sem(f"a_x_first{n}_in") for n in range(NW // 2)]
        x_in = [sem("a_x_in0"), sem("a_x_in1")]
        ident_in, w_in, consts_in, tab_in, raw_in = (sem(f"a_{n}_in") for n in ("ident", "w", "consts", "tab", "raw"))
        shared_in, qkv_in = sem("a_shared_in"), sem("a_wqkv_in")
        x1_out = [sem("a_x1_out0"), sem("a_x1_out1")]
        w_out, tab_out, zero_out = sem("a_w_out"), sem("a_tab_out"), sem("a_zero_out")
        s_half, s_tab, s_xbo = sem("a_half_set"), sem("a_tab_done"), sem("a_xbo_done")
        s_rawh, s_rawl = sem("a_raw_h_done"), sem("a_raw_l_done")
        p_xT, xT_done = sem("a_x_turned"), sem("a_xT_done")
        p_qk, q_done, k_done = sem("a_qk_product"), sem("a_q_done"), sem("a_k_done")
        h_qk, l_qk = sem("a_qk_h_done"), sem("a_qk_l_done")
        p_v, v_done = sem("a_v_product"), sem("a_v_done")
        p_s, s_low, s_exp = sem("a_score_done"), sem("a_low_done"), sem("a_exp_done")
        p_pT, pT_done = sem("a_p_turned"), sem("a_pT_done")
        s_z0, p_z, s_rinv, z_done = sem("a_z_cleared"), sem("a_z_product"), sem("a_rinv_done"), sem("a_z_done")
        p_zT, zT_done = sem("a_z_turned"), sem("a_zT_done")
        p_y, y_done = sem("a_y_product"), sem("a_y_done")
        s_mv = sem("a_mv_done")
        s_ve, s_rstd, x1_done = sem("a_vareps_done"), sem("a_rstd_done"), sem("a_x1_done")

        block = ctx.enter_context(nc.Block())

        def evacs(j):
            return (j + 1 + 3) // 4

        before = [sum(evacs(m) for m in range(j)) for j in range(NW + 1)]
        PER = before[NW]

        FIRST = {0: ("v", 1), 2: ("x", 0), 3: ("x", 2)}
        SECOND = {2: ("x", 1), 3: ("x", 3), 4: ("qk", 0), 5: ("qk", 1), 7: ("v", 0)}
        SPLIT_STEPS = (1, 2, 3, 6)
        PIECES_PER = {"p": PER, "x": NW // 2, "qk": 2, "v": 2}
        ring = []
        for j in range(NW):
            ring += [("p", before[j] + n) for n in range(evacs(j))]
            ring += [fill[j] for fill in (FIRST, SECOND) if j in fill]
        assert len(ring) % 2 == 0
        bank_of = {piece: turn[n % 2] for n, piece in enumerate(ring)}

        def piece_count(kind, n, b):
            target = b if kind == "p" or (kind, n) == ("v", 1) else b + 1
            return target * PIECES_PER[kind] + n + 1

        def exists(kind, n, b):
            if not isinstance(b, int):
                return True
            if kind == "p" or (kind, n) == ("v", 1):
                return 0 <= b < B
            return -1 <= b < B - 1

        def steps(engine, step):
            for b in range(2):
                for j in range(NW):
                    step(b, b, j)
            with engine.Fori(1, B // 2 - 1) as i:
                for parity in range(2):
                    for j in range(NW):
                        step(2 * i + parity, parity, j)
            for b in range(B - 2, B):
                for j in range(NW):
                    step(b, b % 2, j)
            for j in range(3):
                step(B, 0, j)

        def tile(b, off):
            if isinstance(b, int) and not 0 <= NW * b + off < B * NW:
                return None
            return Tile(b, off, 0)

        def fill_of(fill, b, j):
            piece = fill.get(j)
            return piece if piece and exists(*piece, b) and not (isinstance(b, int) and b >= B) else None

        def parity_of(parity, t):
            return (parity + t.off // NW) % 2

        def target_parity(parity, piece):
            return parity if piece == ("v", 1) else 1 - parity

        prelude = [("x", 0), ("x", 1), ("x", 2), ("x", 3), ("qk", 0), ("qk", 1), ("v", 0)]

        @block.sync
        def _(sp):
            sp.dma_start(ident[:], eye).then_inc(ident_in, 16)
            for n in range(NW // 2):
                sp.dma_start(x_nat[:, 0, 2 * n:2 * n + 2],
                             x[2 * n * P:(2 * n + 2) * P, :].rearrange("(t p) e -> p t e", p=P)).then_inc(x0_in[n], 16)
            sp.dma_start(wqk_s[:], wqk).then_inc(w_in, 16)
            sp.dma_start(wv_s[:], wv).then_inc(w_in, 16)
            sp.dma_start(bqk_s[:], bqk).then_inc(consts_in, 16)
            sp.dma_start(bvo_s[:], bvo.partition_broadcast(P)).then_inc(consts_in, 16)
            sp.dma_start(cm[:], cmask).then_inc(consts_in, 16)
            sp.dma_start(wo_s[:], wo0).then_inc(consts_in, 16)
            sp.dma_start(x_nat[:, 1], x[S:2 * S, :].rearrange("(t p) e -> p t e", p=P)).then_inc(x_in[1], 16)
            sp.dma_start(raw[:], w_all[:, 0:WCH]).then_inc(raw_in, 16)
            sp.dma_start(tab[:], tab_base).then_inc(tab_in, 16)
            for layer in range(DEPTH):
                sp.dma_start(tsc[:, layer], tab_scale[layer].partition_broadcast(P)).then_inc(tab_in, 16)
            sp.dma_start(shared["mask"][:], masks).then_inc(shared_in, 16)
            sp.dma_start(shared["par_s"][:], par).then_inc(shared_in, 16)
            for layer in range(DEPTH):
                sp.dma_start(shared["b2_s"][:, layer], b2[layer].partition_broadcast(P)).then_inc(shared_in, 16)
            sp.dma_start(x_d.rearrange("(b r) e -> b r e", r=ROWS)[:, 0, :], zrow).then_inc(zero_out, 16)
            sp.dma_start(mid_d.rearrange("(b r) e -> b r e", r=ROWS)[:, 0, :], zrow[0:B, 0:P]).then_inc(zero_out, 16)

            def step(b, parity, j):
                t = tile(b, j - 3)
                if t:
                    n = t.slot(2)
                    sp.wait_ge(x1_done, t.done(1, 1))
                    sp.dma_start(x_d[bass.ds(t.batch * ROWS + 1 + t.window * P, P), :], x1[:, n]).then_inc(x1_out[n], 16)
                if isinstance(b, int) and b >= B:
                    return
                if isinstance(b, int) and 0 <= NW * (b - (B - 2)) + j - 1 < QKV_PARTS:
                    n = NW * (b - (B - 2)) + j - 1
                    if n == 0:
                        sp.wait_ge(w_out, 128 * b)
                    c = slice(n * O_WO // QKV_PARTS, (n + 1) * O_WO // QKV_PARTS)
                    sp.dma_start(shared["wq_h"][:, c].bitcast(F32), wh_d[:, c]).then_inc(qkv_in, 16)
                    sp.dma_start(shared["wq_l"][:, c].bitcast(F32), wl_d[:, c]).then_inc(qkv_in, 16)
                if j - 1 in SPLIT_STEPS:
                    n = SPLIT_STEPS.index(j - 1)
                    at, c = b * WCH + n * WPART, slice(n * WPART, (n + 1) * WPART)
                    sp.wait_ge(s_rawl, 4 * b + n + 1)
                    sp.dma_start(wh_d[:, bass.ds(at, WPART)], raw_h[:, c].bitcast(F32)).then_inc(w_out, 16)
                    sp.dma_start(wl_d[:, bass.ds(at, WPART)], raw_l[:, c].bitcast(F32)).then_inc(w_out, 16)
                    if not (isinstance(b, int) and b + 1 >= B):
                        sp.dma_start(raw[:, c], w_all[:, bass.ds(at + WCH, WPART)]).then_inc(raw_in, 16)
                if j % 2 and not (isinstance(b, int) and b + 2 >= B):
                    sp.wait_ge(s_xbo, b * NW + j + 1)
                    sp.dma_start(x_nat[:, parity, j - 1:j + 1],
                                 x[bass.ds((b + 2) * S + (j - 1) * P, 2 * P), :].rearrange("(t p) e -> p t e", p=P))\
                        .then_inc(x_in[parity], 16)

            steps(sp, step)
            sp.wait_ge(s_tab, DEPTH * NW)
            sp.dma_start(tab_d, tab1[:]).then_inc(tab_out, 16)
            for j in range(2):
                sp.wait_ge(x1_out[j], 16 * B * NW // 2)
            sp.wait_ge(w_out, 128 * B)
            sp.wait_ge(tab_out, 16)
            sp.wait_ge(zero_out, 32)
            sp.wait_ge(shared_in, 16 * (2 + DEPTH))
            sp.wait_ge(qkv_in, 32 * QKV_PARTS)

        def x_arrived(engine, b, parity, n=None):
            if isinstance(b, int) and b == 0:
                for m in range(NW // 2) if n is None else [n]:
                    engine.wait_ge(x0_in[m], 16)
            elif parity == 1:
                engine.wait_ge(x_in[1], 32 * (b - 1) + 16)
            else:
                engine.wait_ge(x_in[0], 32 * b)

        @block.gpsimd
        def _(pool):
            pool.memset(half[:], -0.5).then_inc(s_half, 1)
            pool.wait_ge(s_half, 1)

            def qk_low(piece, b, parity):
                n = piece[1]
                c, to = slice(n * 512, (n + 1) * 512), target_parity(parity, piece)
                count = piece_count("qk", n, b)
                pool.wait_ge(h_qk, 2 * count)
                pool.tensor_tensor(qT_l[:, to, c], qf[:], qT_h[:, to, c].bitcast(F32), ALU.subtract).then_inc(l_qk, 1)
                pool.tensor_tensor(kT_l[:, to, c], kf[:], kT_h[:, to, c].bitcast(F32), ALU.subtract).then_inc(l_qk, 1)

            for piece in prelude:
                if piece[0] == "qk":
                    qk_low(piece, -1, 1)
            pool.wait_ge(consts_in, 64)

            def step(b, parity, j):
                t = tile(b, j)
                if t:
                    if j == 0:
                        x_arrived(pool, b, parity)
                    need(pool, y_done, t.done(1, -3))
                    pool.tensor_tensor(x_bo[:, j % 4], x_nat[:, parity, j], bvo_s[:, D:D + E], ALU.add)\
                        .then_inc(s_xbo, 1)
                if isinstance(b, int) and b < DEPTH:
                    if j == 0 and b == 0:
                        pool.wait_ge(tab_in, 16 * (1 + DEPTH))
                    to = rope[:, j].rearrange("p c d -> p (c d)") if b == 0 else tab1[:, j]
                    pool.tensor_tensor(to, tab[:, j], tsc[:, b], ALU.mult).then_inc(s_tab, 1)
                if j in SPLIT_STEPS and not (isinstance(b, int) and b >= B):
                    n = SPLIT_STEPS.index(j)
                    c = slice(n * WPART, (n + 1) * WPART)
                    pool.wait_ge(s_rawh, 4 * b + n + 1)
                    need(pool, w_out, 128 * b)
                    pool.tensor_tensor(raw_l[:, c], raw[:, c], raw_h[:, c].bitcast(F32), ALU.subtract)\
                        .then_inc(s_rawl, 1)
                t = tile(b, j - 2)
                if t:
                    n = t.window
                    pool.wait_ge(s_ve, t.done(1, 1))
                    pool.tensor_tensor(rstd[:, n:n + 1], mv[:, n, 1:2], half[:], ALU.pow).then_inc(s_rstd, 1)
                fill = fill_of(SECOND, b, j)
                if fill and fill[0] == "qk":
                    qk_low(fill, b, parity)

            steps(pool, step)

        @block.scalar
        def _(act):
            def fill_high(piece, b, parity):
                kind, n = piece
                count, to, bank = piece_count(kind, n, b), target_parity(parity, piece), bank_of[piece]
                if kind == "x":
                    act.wait_ge(p_xT, count)
                    act.activation(xT[:, :, n * 256:(n + 1) * 256], bank[:].rearrange("p (k t) -> p k t", k=KE),
                                   ACT.Copy).then_inc(xT_done, 1)
                if kind == "qk":
                    c = slice(n * 512, (n + 1) * 512)
                    act.wait_ge(q_done, count)
                    need(act, l_qk, 2 * count - 2)
                    act.activation(kf[:], bank[D:2 * D, :], ACT.Identity, bias=bqk_s[D:2 * D, 0:1]).then_inc(k_done, 1)
                    act.activation(qT_h[:, to, c], qf[:], ACT.Copy).then_inc(h_qk, 1)
                    act.wait_ge(k_done, count)
                    act.activation(kT_h[:, to, c], kf[:], ACT.Copy).then_inc(h_qk, 1)

            def probabilities(t):
                j = t.window
                act.wait_ge(s_low, t.done(1, 1))
                act.activation(prob[:, j % 4, 0:(j + 1) * P], prob[:, j % 4, 0:(j + 1) * P], ACT.Exp,
                               bias=low[:, j:j + 1], scale=-1.0, accum_out=rsum[:, j:j + 1]).then_inc(s_exp, 1)

            for piece in prelude:
                if piece == ("qk", 0):
                    act.wait_ge(consts_in, 64)
                fill_high(piece, -1, 1)

            def step(b, parity, j):
                if isinstance(b, int) and b == 0 and j == 0:
                    probabilities(tile(b, 0))
                    probabilities(tile(b, 1))
                t = tile(b, j)
                if t:
                    for n in range(evacs(j)):
                        c0, c1 = 4 * n, min(4 * n + 4, j + 1)
                        act.wait_ge(p_pT, piece_count("p", before[j] + n, b))
                        act.activation(pT[:, j % 2, c0:c1, :],
                                       bank_of["p", before[j] + n][:, 0:(c1 - c0) * P]
                                       .rearrange("p (c t) -> p c t", t=P), ACT.Copy).then_inc(pT_done, 1)
                first, second = fill_of(FIRST, b, j), fill_of(SECOND, b, j)
                t = tile(b, j + 2)
                if t:
                    probabilities(t)
                if first:
                    fill_high(first, b, parity)
                if second:
                    fill_high(second, b, parity)
                if j in SPLIT_STEPS and not (isinstance(b, int) and b >= B):
                    n = SPLIT_STEPS.index(j)
                    c = slice(n * WPART, (n + 1) * WPART)
                    act.wait_ge(raw_in, 64 * b + 16)
                    need(act, w_out, 128 * b)
                    act.activation(raw_h[:, c], raw[:, c], ACT.Copy).then_inc(s_rawh, 1)

            steps(act, step)

        @block.vector
        def _(dve):
            dve.memset(z[:], 0.0).then_inc(s_z0, 1)
            dve.wait_ge(s_z0, 1)

            def fill_done(piece, b, parity):
                kind, n = piece
                count, to, bank = piece_count(kind, n, b), target_parity(parity, piece), bank_of[piece]
                if kind == "qk":
                    dve.wait_ge(p_qk, count)
                    need(dve, l_qk, 2 * count - 2)
                    dve.tensor_scalar(qf[:], bank[0:D, :], bqk_s[0:D, 0:1], -float(D) ** -0.5, ALU.add, ALU.mult)\
                        .then_inc(q_done, 1)
                if kind == "v":
                    dve.wait_ge(p_v, count)
                    dve.tensor_tensor(v[:, to, 4 * n:4 * n + 4], bank[:, 0:4 * D].rearrange("p (t d) -> p t d", d=D),
                                      bvo_s[:, 0:D].unsqueeze(1).to_broadcast([P, 4, D]), ALU.add).then_inc(v_done, 1)

            for piece in prelude:
                if piece == ("qk", 0):
                    dve.wait_ge(consts_in, 64)
                fill_done(piece, -1, 1)

            def softmax_low(t):
                j = t.window
                nk = j + 1
                dve.wait_ge(p_s, t.done(1, 1))
                dve.memset(took[:, j:j + 1], 0.0)
                dve.tensor_tensor_reduce(prob[:, j % 4, 0:nk * P], score[j % 2][:, 0:nk * P], cm[:, S - nk * P:S],
                                         1.0, BIG, ALU.add, ALU.min, low[:, j:j + 1]).then_inc(s_low, 1)

            def step(b, parity, j):
                if isinstance(b, int) and b == 0 and j == 0:
                    softmax_low(tile(b, 0))
                    softmax_low(tile(b, 1))
                first, second = fill_of(FIRST, b, j), fill_of(SECOND, b, j)
                c = tile(b, j - 2)
                if c:
                    dve.wait_ge(p_zT, c.done(1, 1))
                    dve.tensor_copy(zT[:, j % 2], py[0:D, 0:P]).then_inc(zT_done, 1)
                t = tile(b, j + 2)
                if t:
                    softmax_low(t)
                if first:
                    fill_done(first, b, parity)
                a = tile(b, j - 1)
                if a:
                    n = a.window
                    dve.wait_ge(s_exp, a.done(1, 1))
                    dve.reciprocal(rinv[:, n:n + 1], rsum[:, n:n + 1]).then_inc(s_rinv, 1)
                    dve.wait_ge(s_rinv, a.done(1, 1))
                    dve.wait_ge(p_z, a.done(1, 1))
                    dve.tensor_scalar(z[:, n % 2, 0:D], pz[:, 0:D], rinv[:, n:n + 1], None, ALU.mult).then_inc(z_done, 1)
                d = tile(b, j - 3)
                if d:
                    n, m = d.slot(2), d.window
                    dve.wait_ge(s_rstd, d.done(1, 1))
                    need(dve, x1_out[n], 16 * d.uses(2))
                    dve.tensor_scalar(x1[:, n], y[:, n], mv[:, m, 0:1], rstd[:, m:m + 1],
                                      ALU.subtract, ALU.mult).then_inc(x1_done, 1)
                if c:
                    n = c.window
                    dve.wait_ge(p_y, c.done(1, 1))
                    dve.wait_ge(s_xbo, c.done(1, 1))
                    dve.tensor_tensor(y[:, j % 2], py[:, 0:E], x_bo[:, n % 4], ALU.add).then_inc(y_done, 1)
                    dve.wait_ge(y_done, c.done(1, 1))
                    dve.bn_stats(stats[:, n], y[:, j % 2])
                    dve.drain()
                    dve.bn_aggr(mv[:, n], stats[:, n]).then_inc(s_mv, 1)
                    dve.wait_ge(s_mv, c.done(1, 1))
                    dve.tensor_scalar(mv[:, n, 1:2], mv[:, n, 1:2], EPS, None, ALU.add).then_inc(s_ve, 1)
                if second:
                    fill_done(second, b, parity)

            steps(dve, step)

        @block.tensor
        def _(pe):
            pe.wait_ge(ident_in, 16)

            def bank_free(kind, n, b):
                at = ring.index((kind, n))
                while True:
                    at -= 2
                    if at < 0:
                        at, b = at + len(ring), b - 1
                        if isinstance(b, int) and b < -1:
                            return
                    if exists(*ring[at], b):
                        break
                left = {"p": pT_done, "x": xT_done, "qk": k_done, "v": v_done}[ring[at][0]]
                pe.wait_ge(left, piece_count(*ring[at], b))

            def make_fill(piece, b, parity):
                kind, n = piece
                count, bank = piece_count(kind, n, b), bank_of[piece]
                bank_free(kind, n, b)
                if kind == "x":
                    to = target_parity(parity, piece)
                    if n == 0 or (isinstance(b, int) and b == -1):
                        x_arrived(pe, b + 1, to, n)
                    for k in range(KE):
                        for m in range(2):
                            ins = pe.transpose(bank[:, k * 256 + m * P:k * 256 + (m + 1) * P],
                                               x_nat[:, to, 2 * n + m, k * P:(k + 1) * P], ident[:])
                    ins.then_inc(p_xT, 1)
                if kind == "qk":
                    pe.wait_ge(xT_done, (b + 1) * (NW // 2) + 2 * n + 2)
                    c = slice(n * 512, (n + 1) * 512)
                    for k in range(KE):
                        ins = pe.matmul(bank[:], wqk_s[:, k], xT[:, k, c], start=k == 0, stop=k == KE - 1)
                    ins.then_inc(p_qk, 1)
                if kind == "v":
                    for m in range(4):
                        c = slice((4 * n + m) * P, (4 * n + m + 1) * P)
                        for k in range(KE):
                            ins = pe.matmul(bank[:, m * D:(m + 1) * D], xT[:, k, c], wv_s[:, k],
                                            start=k == 0, stop=k == KE - 1)
                    ins.then_inc(p_v, 1)

            def scores(t, parity):
                j, at = t.window, parity_of(parity, t)
                if j == 0 or j == 4:
                    pe.wait_ge(l_qk, 4 * t.batch + 2 * (j // 4) + 2)
                need(pe, s_low, t.done(1, -1))
                cols = slice(j * P, (j + 1) * P)
                for c in range(0, (j + 1) * P, 512):
                    keys = slice(c, min(c + 512, (j + 1) * P))
                    ins = three_pass(pe, score[j % 2][:, keys], (qT_h[:, at, cols], qT_l[:, at, cols]),
                                     (kT_h[:, at, keys], kT_l[:, at, keys]), True, True)
                ins.then_inc(p_s, 1)

            for piece in prelude:
                if piece == ("qk", 0):
                    pe.wait_ge(w_in, 32)
                make_fill(piece, -1, 1)
            pe.wait_ge(consts_in, 64)

            def step(b, parity, j):
                if isinstance(b, int) and b == 0 and j == 0:
                    scores(tile(b, 0), parity)
                    scores(tile(b, 1), parity)
                t = tile(b, j + 2)
                if t:
                    scores(t, parity)
                c = tile(b, j - 2)
                if c:
                    pe.wait_ge(z_done, c.done(1, 1))
                    need(pe, y_done, c.done(1))
                    pe.transpose(py[:, 0:P], z[:, j % 2], ident[:]).then_inc(p_zT, 1)
                t = tile(b, j)
                if t:
                    pe.wait_ge(s_exp, t.done(1, 1))
                    for n in range(evacs(j)):
                        bank_free("p", before[j] + n, b)
                        for k in range(4 * n, min(4 * n + 4, j + 1)):
                            ins = pe.transpose(bank_of["p", before[j] + n][:, (k - 4 * n) * P:(k - 4 * n + 1) * P],
                                               prob[:, j % 4, k * P:(k + 1) * P], ident[:])
                        ins.then_inc(p_pT, 1)
                first, second = fill_of(FIRST, b, j), fill_of(SECOND, b, j)
                if first:
                    make_fill(first, b, parity)
                a = tile(b, j - 1)
                if a:
                    n, at = a.window, parity_of(parity, a)
                    pe.wait_ge(pT_done, a.batch * PER + before[n + 1])
                    if n == 0 or n == 4:
                        pe.wait_ge(v_done, 2 * a.batch + n // 4 + 1)
                    need(pe, z_done, a.done(1))
                    for k in range(n + 1):
                        ins = pe.matmul(pz[:, 0:D], pT[:, n % 2, k, :], v[:, at, k, :], start=k == 0, stop=k == n)
                    ins.then_inc(p_z, 1)
                if c:
                    pe.wait_ge(zT_done, c.done(1, 1))
                    pe.matmul(py[:, 0:E], zT[:, j % 2], wo_s[:], start=True, stop=True).then_inc(p_y, 1)
                if second:
                    make_fill(second, b, parity)

            steps(pe, step)


class Tile:

    def __init__(self, i, off, layer):
        self.i, self.off, self.layer = i, off, layer
        self.window = off % NW
        self.batch = i + off // NW
        self.first = self.window == 0

    def done(self, per, more=0):
        return per * NW * self.i + per * self.off + more

    def slot(self, ring):
        return self.off % ring

    def uses(self, ring, more=0):
        return NW // ring * self.i + self.off // ring + more

    def is_number(self, n):
        return isinstance(self.i, int) and NW * self.i + self.off == n


TILES = DEPTH * B * NW
LAYER = B * NW
LAG_MAX = 5


class Step:
    def __init__(self, i, w, layer=None):
        self.i, self.w, self.layer = i, w, layer
        self.even = w % 2 == 0

    def tile(self, lag):
        off = self.w - lag
        if isinstance(self.i, int):
            g = NW * self.i + off
            return Tile(self.i, off, g // LAYER) if 0 <= g < TILES else None
        return Tile(self.i, off, self.layer)


def all_steps(engine, step, peel_last=False):
    last = DEPTH * B - (1 if peel_last else 0)
    for w in range(NW):
        step(Step(0, w))
    with engine.Fori(1, B) as i:
        for w in range(NW):
            step(Step(i, w, 0))
    for w in range(NW):
        step(Step(B, w))
    with engine.Fori(B + 1, last) as i:
        for w in range(NW):
            step(Step(i, w, 1))
    if peel_last:
        for w in range(NW):
            step(Step(last, w))
    for w in range(LAG_MAX):
        step(Step(DEPTH * B, w))


def layers_phase(nc, x_d, mid_d, wh_d, wl_d, tab_d, out, shared):
    with ExitStack() as ctx:
        def sb(name, shape, dt=F32):
            return ctx.enter_context(nc.sbuf_tensor(name, shape, dt))

        def ps(name, shape):
            return ctx.enter_context(nc.psum_tensor(name, shape, F32))

        def sem(name):
            return ctx.enter_context(nc.semaphore(name))

        wh, wl = sb("w_h", [P, NWC - O_WO], F32R), sb("w_l", [P, NWC - O_WO], F32R)
        tab, b2_s, par_s, mask, ident = (shared[n] for n in ("rope", "b2_s", "par_s", "mask", "ident"))
        half, eps = sb("minus_half", [P, 2 * H]), sb("eps", [P, 1])
        took = sb("wait_taker", [1, 4])
        x_sb = sb("x_tile", [P, 4, E + P])
        xT_h, xT_l = sb("xT_h", [P, KE, P], F32R), sb("xT_l", [P, KE, P], F32R)
        sq = sb("squares", [P, 2 * H, D])
        ss = sb("norms_sq", [P, 2 * H])
        r = sb("inv_norm", [P, 2, 2 * H])
        rt = sb("norm_clipped", [P, 2 * H])
        rope_a, rope_b = sb("rope_cos", [P, 2, H, D]), sb("rope_sin", [P, 2, H, D])
        qn, kn = sb("q_rot", [P, INNER]), sb("k_rot", [P, INNER])
        qT_h, qT_l = sb("qT_h", [P, H // 2, P], F32R), sb("qT_l", [P, H // 2, P], F32R)
        kT_h, kT_l = sb("kT_h", [P, H // 2, 2, P], F32R), sb("kT_l", [P, H // 2, 2, P], F32R)
        v = sb("v", [P, 4, INNER])
        prob = sb("prob", [P, H, 2 * P])
        least = sb("least", [P, H])
        rsum, rinv = sb("rsum", [P, H]), sb("rinv", [P, H])
        pT = sb("pT", [P, 2, 4, 2, P])
        o = sb("o", [P, INNER])
        oT_h, oT_l = sb("oT_h", [P, INNER // P, P], F32R), sb("oT_l", [P, INNER // P, P], F32R)
        mid = sb("x_mid", [P, 2, E])
        shifted = sb("x_mid_shifted", [P, 2, P])
        res = sb("residual", [P, 4, E])
        st = sb("ln_stats", [P, 2, 2, 6])
        mv = sb("ln_mean_var", [P, 2, 2])
        ve, rstd = sb("ln_var_eps", [P, 2]), sb("ln_rstd", [P, 2])
        hn = sb("h_norm", [P, 2, E])
        hv = sb("hT", [P, KE, 2 * P])
        hT_h, hT_l = sb("hT_h", [P, KE, 2 * P], F32R), sb("hT_l", [P, KE, 2 * P], F32R)
        gel, gt = sb("gelu", [P, 2, 2 * P]), sb("gated", [P, 3, 2 * P])
        gT_h, gT_l = sb("gT_h", [P, HF + 1, 2 * P], F32R), sb("gT_l", [P, HF + 1, 2 * P], F32R)
        xf = sb("x_new", [P, 2, E])
        x1 = sb("x1_tile", [P, 2, E])
        fst, fmv = sb("f_stats", [P, 2, 6]), sb("f_mean_var", [P, 2, 2])
        fve, frstd = sb("f_var_eps", [P, 2]), sb("f_rstd", [P, 2])
        fo = sb("out_tile", [P, 2, E])

        p_score = [ps("p_score0", [P, 512]), ps("p_score1", [P, 512])]
        p_turn = [ps("p_turn0", [P, 512]), ps("p_turn1", [P, 512])]
        p_wide = [ps("p_wide0", [P, 512]), ps("p_wide1", [P, 512])]
        p_val = ps("p_values", [P, 512])
        p_mix = ps("p_mixed", [P, 512])

        w_in = {n: sem(f"w_{n}_in") for n in ("qkv", "wo", "w1", "w2")}
        tab_in = sem("tab_in")
        x_in = [sem(f"x_in{n}") for n in range(4)]
        x1_in = [sem(f"x1_in{n}") for n in range(2)]
        mid_out = [sem(f"mid_out{n}") for n in range(2)]
        shifted_in = [sem(f"shifted_in{n}") for n in range(2)]
        x_out = [sem(f"x_out{n}") for n in range(2)]
        out_out = [sem(f"out_out{n}") for n in range(2)]
        pe_qT, pe_kT, pe_xT, pe_oT, pe_hT = (sem(f"pe_{n}_turned") for n in ("q", "k", "x", "o", "h"))
        pe_q, pe_k, pe_v = (sem(f"pe_{n}_product") for n in ("q", "k", "v"))
        pe_s, pe_pT, pe_pv = sem("pe_scores"), sem("pe_p_turned"), sem("pe_values")
        pe_wo, pe_w1, pe_w2 = sem("pe_wo"), sem("pe_w1"), sem("pe_w2")
        act_qT, act_kT, act_xT, act_oT, act_hT = (sem(f"act_{n}T_h") for n in ("q", "k", "x", "o", "h"))
        act_sq = [sem("act_q_squares"), sem("act_k_squares")]
        act_v, act_exp, act_pT = sem("act_v"), sem("act_exp"), sem("act_pT")
        act_gelu, act_gT = sem("act_gelu"), sem("act_gT_h")
        dve_qT, dve_kT, dve_xT, dve_oT, dve_hT = (sem(f"dve_{n}T_l") for n in ("q", "k", "x", "o", "h"))
        dve_least, dve_qr, dve_kr = sem("dve_least"), sem("dve_q_rope"), sem("dve_k_rope")
        dve_ss = [sem("dve_q_norms_sq"), sem("dve_k_norms_sq")]
        dve_rt = [sem("dve_q_clip"), sem("dve_k_clip")]
        dve_rinv, dve_o, dve_mid = sem("dve_rinv"), sem("dve_o"), sem("dve_mid")
        dve_mv, dve_hn, dve_hv = sem("dve_mean_var"), sem("dve_h_norm"), sem("dve_hT")
        dve_gt, dve_gT = sem("dve_gated"), sem("dve_gT_l")
        dve_x, dve_fmv, dve_out = sem("dve_x_new"), sem("dve_f_mean_var"), sem("dve_out")
        pool_half = sem("pool_half")
        pool_ve, pool_rstd, pool_fve, pool_frstd = (sem(f"pool_{n}") for n in ("ve", "rstd", "fve", "frstd"))
        pool_r1, pool_res = sem("pool_residual_part"), sem("pool_residual")
        dve_q = sem("dve_q_sum")
        pool_ka, pool_k = sem("pool_k_sum"), sem("pool_k")
        pool_r = [sem("pool_q_inv_norm"), sem("pool_k_inv_norm")]

        block = ctx.enter_context(nc.Block())

        w_at = {"qkv": (O_QKV, O_WO), "wo": (O_WO, O_W1), "w1": (O_W1, O_W2), "w2": (O_W2, NWC)}

        def weight_at(name):
            if name == "qkv":
                return shared["wq_h"][:], shared["wq_l"][:]
            a, b = (c - O_WO for c in w_at[name])
            return wh[:, a:b], wl[:, a:b]

        def weight(name, chunks):
            return tuple(t.rearrange("p (k n) -> p k n", k=chunks) for t in weight_at(name))

        wqkv, wo, w1, w2 = (weight("qkv", KE), weight("wo", INNER // P), weight("w1", KE), weight("w2", HF + 1))

        def blocks_of(t):
            own = t.slot(2)
            return [own] if t.first else [1 - own, own]

        def key_columns(t):
            own = t.slot(2)
            return slice(own * P, own * P + P) if t.first else slice(0, 2 * P)

        def pair_done(t, per, more=0):
            return per * (NW // 2) * t.i + per * (t.off // 2) + more

        @block.sync
        def _(sp):
            def load_weights(name, layer):
                a, b = w_at[name]
                c = layer * NWC
                for to, source in zip(weight_at(name), (wh_d, wl_d)):
                    sp.dma_start(to.bitcast(F32), source[:, c + a:c + b]).then_inc(w_in[name], 16)

            def load_x(t):
                row = t.batch * ROWS + 1 + t.window * P
                n = t.slot(4)
                sp.dma_start(x_sb[:, n, 0:E], x_d[bass.ds(row, P), :]).then_inc(x_in[n], 16)
                sp.dma_start(x_sb[:, n, E:E + P], x_d[bass.ds(row - 1, P), P:E]).then_inc(x_in[n], 16)

            load_x(Tile(0, 0, 0))
            load_x(Tile(0, 1, 0))
            load_weights("wo", 0)
            load_weights("w1", 0)
            load_weights("w2", 0)

            def step(st_):
                if st_.i is not None and isinstance(st_.i, int) and st_.i == B:
                    if st_.w == 0:
                        sp.wait_ge(pe_v, LAYER)
                        load_weights("qkv", 1)
                        sp.wait_ge(dve_qr, LAYER)
                        sp.dma_start(tab[:], tab_d.rearrange("p (w c d) -> p w c d", w=NW, c=4)).then_inc(tab_in, 16)
                    if st_.w == 2:
                        sp.wait_ge(pe_wo, LAYER)
                        load_weights("wo", 1)
                    if st_.w == 4:
                        sp.wait_ge(pe_w1, (HF + 1) * LAYER // 2)
                        load_weights("w1", 1)
                    if st_.w == 5:
                        sp.wait_ge(pe_w2, LAYER)
                        load_weights("w2", 1)
                t = st_.tile(1)
                if t and t.layer == 1:
                    need(sp, pool_res, t.done(1, -1))
                    row = (t.batch - B) * ROWS + 1 + t.window * P
                    sp.dma_start(x1[:, t.slot(2)], x_d[bass.ds(row, P), :]).then_inc(x1_in[t.slot(2)], 16)
                t = st_.tile(3)
                if t:
                    need(sp, mid_out[t.slot(2)], 16 * t.uses(2, 1))
                    prev = Tile(t.i, t.off - 1, t.layer)
                    need(sp, mid_out[prev.slot(2)], 16 * prev.uses(2, 1))
                    row = mid_row(t) - 1
                    sp.dma_start(shifted[:, t.slot(2)], mid_d[bass.ds(row, P), :]).then_inc(shifted_in[t.slot(2)], 16)
                t = st_.tile(5)
                if t and t.layer == 0:
                    sp.wait_ge(dve_x, t.done(1, 1))
                    row = (t.batch + B) * ROWS + 1 + t.window * P
                    sp.dma_start(x_d[bass.ds(row, P), :], xf[:, t.slot(2)]).then_inc(x_out[t.slot(2)], 16)
                t = st_.tile(2)
                if t:
                    sp.wait_ge(dve_mid, t.done(1, 1))
                    sp.dma_start(mid_d[bass.ds(mid_row(t), P), :], mid[:, t.slot(2), P:E])\
                        .then_inc(mid_out[t.slot(2)], 16)
                t = st_.tile(-2)
                if t:
                    need(sp, dve_mid, t.done(1, -3))
                    if t.layer == 1:
                        for back in (0, 1):
                            src = Tile(t.i - B, t.off - back, 0)
                            need(sp, x_out[src.slot(2)], 16 * src.uses(2, 1))
                    load_x(t)
                t = st_.tile(5)
                if t and t.layer == 1:
                    sp.wait_ge(dve_out, t.done(1, 1 - LAYER))
                    row = (t.batch - B) * S + t.window * P
                    sp.dma_start(out[bass.ds(row, P), :], fo[:, t.slot(2)]).then_inc(out_out[t.slot(2)], 16)

            def mid_row(t):
                return (t.batch - t.layer * B) * ROWS + 1 + t.window * P

            all_steps(sp, step, peel_last=True)
            for n in range(2):
                sp.wait_ge(out_out[n], 16 * LAYER // 2)
                sp.wait_ge(x_out[n], 16 * LAYER // 2)
                sp.wait_ge(mid_out[n], 16 * TILES // 2)

        @block.gpsimd
        def _(pool):
            pool.memset(half[:], -0.5)
            pool.memset(eps[:], EPS).then_inc(pool_half, 1)
            pool.wait_ge(pool_half, 1)
            def step(st_):
                t = st_.tile(5)
                if t and t.layer == 1:
                    n = t.slot(2)
                    pool.wait_ge(dve_fmv, t.done(1, 1 - LAYER))
                    pool.tensor_tensor(fve[:, n:n + 1], fmv[:, n, 1:2], eps[:, 0:1], ALU.add).then_inc(pool_fve, 1)
                    pool.wait_ge(pool_fve, t.done(1, 1 - LAYER))
                    pool.tensor_tensor(frstd[:, n:n + 1], fve[:, n:n + 1], half[:, 0:1], ALU.pow).then_inc(pool_frstd, 1)
                t = st_.tile(3)
                if t:
                    n = t.slot(2)
                    pool.wait_ge(dve_mv, t.done(1, 1))
                    pool.tensor_tensor(ve[:, n:n + 1], mv[:, n, 1:2], eps[:, 0:1], ALU.add).then_inc(pool_ve, 1)
                    pool.wait_ge(pool_ve, t.done(1, 1))
                    pool.tensor_tensor(rstd[:, n:n + 1], ve[:, n:n + 1], half[:, 0:1], ALU.pow).then_inc(pool_rstd, 1)
                t = st_.tile(2)
                if t:
                    pool.wait_ge(dve_mid, t.done(1, 1))
                    need(pool, dve_x, t.done(1, -3))
                    n = t.slot(4)
                    if t.layer == 0:
                        pool.tensor_tensor(res[:, n], mid[:, t.slot(2)], b2_s[:, 0], ALU.add).then_inc(pool_res, 1)
                    else:
                        pool.tensor_tensor(res[:, n], mid[:, t.slot(2)], b2_s[:, 1], ALU.add).then_inc(pool_r1, 1)
                        pool.wait_ge(x1_in[t.slot(2)], 16 * t.uses(2, 1 - LAYER // 2))
                        pool.wait_ge(pool_r1, t.done(1, 1 - LAYER))
                        pool.tensor_tensor(res[:, n], res[:, n], x1[:, t.slot(2)], ALU.add).then_inc(pool_res, 1)
                t = st_.tile(0)
                if t:
                    slot = t.slot(2)

                    def inverse_norms(n):
                        heads = slice(n * H, (n + 1) * H)
                        pool.wait_ge(dve_rt[n], t.done(1, 1))
                        pool.tensor_tensor(r[:, slot, heads], rt[:, heads], half[:, heads], ALU.pow)\
                            .then_inc(pool_r[n], 1)

                    pool.wait_ge(dve_kr, t.done(1, 1))
                    pool.tensor_tensor(rope_a[:, 1], rope_a[:, 1], rope_b[:, 1], ALU.add).then_inc(pool_ka, 1)
                    inverse_norms(1)
                    pool.wait_ge(pool_r[1], t.done(1, 1))
                    pool.wait_ge(pool_ka, t.done(1, 1))
                    need(pool, pe_kT, t.done(1))
                    pool.tensor_tensor(kn[:].rearrange("p (h d) -> p h d", h=H), rope_a[:, 1],
                                       r[:, slot, H:2 * H].unsqueeze(2).to_broadcast([P, H, D]), ALU.mult)\
                        .then_inc(pool_k, 1)
                    inverse_norms(0)

            all_steps(pool, step)

        @block.scalar
        def _(act):
            def step(st_):
                t, u = st_.tile(0), st_.tile(-1)

                def turned_x(u):
                    act.wait_ge(pe_xT, u.done(1, 1))
                    act.activation(xT_h[:], p_mix[:, 0:E].rearrange("p (k t) -> p k t", k=KE), ACT.Copy).then_inc(act_xT, 1)

                if t and t.is_number(0):
                    turned_x(t)
                a = st_.tile(1)
                if a:
                    act.wait_ge(pe_qT, a.done(1, 1))
                    act.activation(qT_h[:], p_turn[0][:].rearrange("p (c t) -> p c t", t=P), ACT.Copy).then_inc(act_qT, 1)
                    act.wait_ge(pe_kT, a.done(1, 1))
                    act.activation(kT_h[:, :, a.slot(2), :], p_turn[1][:].rearrange("p (c t) -> p c t", t=P), ACT.Copy)\
                        .then_inc(act_kT, 1)
                c = st_.tile(2)
                if c:
                    act.wait_ge(pe_oT, c.done(1, 1))
                    act.activation(oT_h[:], p_val[:].rearrange("p (k t) -> p k t", t=P), ACT.Copy).then_inc(act_oT, 1)

                def probabilities(first, last):
                    cols = key_columns(a)
                    for h in range(first, last):
                        act.wait_ge(dve_least, a.done(H, h + 1))
                        act.activation(prob[:, h, cols], prob[:, h, cols], ACT.Exp, bias=least[:, h:h + 1],
                                       scale=-1.0, accum_out=rsum[:, h:h + 1]).then_inc(act_exp, 1)

                def squares(n, product):
                    act.wait_ge(product, t.done(1, 1))
                    need(act, dve_ss[n], t.done(1))
                    act.activation(sq[:, n * H:(n + 1) * H], p_wide[1 - n][:].rearrange("p (h d) -> p h d", h=H),
                                   ACT.Square).then_inc(act_sq[n], 1)

                def turned_probs(group):
                    own = blocks_of(a)
                    for n in range(2):
                        act.wait_ge(pe_pT, a.done(4, 2 * group + n + 1))
                        src = p_turn[n][:].rearrange("p (h b t) -> p h b t", h=2, b=2)
                        act.activation(pT[:, group, 2 * n:2 * n + 2, own[0] if a.first else slice(0, 2), :],
                                       src[:, :, own[0] if a.first else slice(0, 2), :], ACT.Copy).then_inc(act_pT, 1)

                if a:
                    probabilities(0, 4)
                if t:
                    squares(1, pe_k)
                if a:
                    turned_probs(0)
                    probabilities(4, 6)
                if t:
                    squares(0, pe_q)
                if a:
                    probabilities(6, 8)
                    turned_probs(1)
                f = st_.tile(4)
                if st_.even and f:
                    act.wait_ge(dve_hv, pair_done(f, 1, 1))
                    act.activation(hT_h[:], hv[:], ACT.Copy).then_inc(act_hT, 1)
                if t:
                    act.wait_ge(pe_v, t.done(1, 1))
                    act.activation(v[:, t.slot(4)], p_wide[0][:], ACT.Copy).then_inc(act_v, 1)
                if u and not (st_.even and f):
                    turned_x(u)
                if st_.even and f:
                    def gate(n):
                        act.wait_ge(pe_w1, pair_done(f, HF + 1, n + 1))
                        need(act, dve_gt, pair_done(f, HF + 1, n - 1))
                        bank = p_wide[(n + 1) % 2]
                        col = 2 * KE + HF + n
                        if n < HF:
                            act.activation(gel[:, n % 2], bank[:, 2 * P:4 * P], ACT.Gelu,
                                           bias=par_s[:, f.layer, col:col + 1]).then_inc(act_gelu, 1)
                        else:
                            act.activation(gel[0:HR, n % 2], bank[GR:GR + HR, 0:2 * P], ACT.Gelu,
                                           bias=par_s[GR:GR + HR, f.layer, col:col + 1]).then_inc(act_gelu, 1)

                    def high(n):
                        rows = P if n < HF else HR
                        act.wait_ge(dve_gt, pair_done(f, HF + 1, n + 1))
                        act.activation(gT_h[0:rows, n], gt[0:rows, n % 3], ACT.Copy).then_inc(act_gT, 1)

                    gate(0)
                    for n in range(1, HF + 1):
                        gate(n)
                        high(n - 1)
                        if u and n == 1:
                            turned_x(u)
                    high(HF)

            all_steps(act, step, peel_last=True)

        @block.vector
        def _(dve):
            def step(st_):
                a, t, c, g, e = (st_.tile(n) for n in (1, 0, 2, 3, 5))
                u, f = st_.tile(-1), st_.tile(4)

                def turned_x(u):
                    dve.wait_ge(act_xT, u.done(1, 1))
                    dve.tensor_tensor(xT_l[:], p_mix[:, 0:E].rearrange("p (k t) -> p k t", k=KE),
                                      xT_h[:].bitcast(F32), ALU.subtract).then_inc(dve_xT, 1)

                if t and t.is_number(0):
                    turned_x(t)
                if a:
                    dve.wait_ge(act_qT, a.done(1, 1))
                    dve.tensor_tensor(qT_l[:], p_turn[0][:].rearrange("p (c t) -> p c t", t=P),
                                      qT_h[:].bitcast(F32), ALU.subtract).then_inc(dve_qT, 1)
                    dve.wait_ge(act_kT, a.done(1, 1))
                    dve.tensor_tensor(kT_l[:, :, a.slot(2), :], p_turn[1][:].rearrange("p (c t) -> p c t", t=P),
                                      kT_h[:, :, a.slot(2), :].bitcast(F32), ALU.subtract).then_inc(dve_kT, 1)
                if c:
                    dve.wait_ge(act_oT, c.done(1, 1))
                    dve.tensor_tensor(oT_l[:], p_val[:].rearrange("p (k t) -> p k t", t=P),
                                      oT_h[:].bitcast(F32), ALU.subtract).then_inc(dve_oT, 1)
                if e:
                    n = e.slot(2)
                    dve.wait_ge(pe_w2, e.done(1, 1))
                    dve.wait_ge(pool_res, e.done(1, 1))
                    if e.layer == 0:
                        need(dve, x_out[n], 16 * e.uses(2))
                    elif e.is_number(LAYER) or e.is_number(LAYER + 1):
                        dve.wait_ge(x_out[n], 16 * LAYER // 2)
                    dve.tensor_tensor(xf[:, n], p_mix[:, 0:E], res[:, e.slot(4)], ALU.add).then_inc(dve_x, 1)
                    if e.layer == 1:
                        dve.wait_ge(dve_x, e.done(1, 1))
                        dve.bn_stats(fst[:, n], xf[:, n])
                if g:
                    n = g.slot(2)
                    dve.wait_ge(shifted_in[n], 16 * g.uses(2, 1))
                    dve.bn_stats(st[:, n, 0], mid[:, n, 0:P])
                    dve.bn_stats(st[:, n, 1], shifted[:, n])
                final = e and e.layer == 1
                if g or final:
                    dve.drain()
                if g:
                    dve.bn_aggr(mv[:, g.slot(2)], st[:, g.slot(2)]).then_inc(dve_mv, 1)
                if final:
                    dve.bn_aggr(fmv[:, e.slot(2)], fst[:, e.slot(2)]).then_inc(dve_fmv, 1)

                def least_of(group):
                    cols = key_columns(a)
                    dve.wait_ge(pe_s, a.done(2, group + 1))
                    if group == 0:
                        dve.wait_ge(pool_r[0], a.done(1, 1))
                    at = 2 * a.slot(2) + group
                    dve.memset(took[:, at:at + 1], 0.0)
                    for h in range(4 * group, 4 * group + 4):
                        c0 = h % 4 // 2 * 2 * P
                        dve.tensor_tensor_reduce(prob[:, h, cols], p_score[h % 2][:, c0 + cols.start:c0 + cols.stop],
                                                 mask[:, a.slot(2), cols], r[:, a.slot(2), h:h + 1], BIG,
                                                 ALU.add, ALU.min, least[:, h:h + 1]).then_inc(dve_least, 1)

                def rotary(n, raised, last):
                    dve.wait_ge(act_sq[n], t.done(1, 1))
                    need(dve, last, t.done(1))
                    if n == 1 and t.is_number(LAYER):
                        dve.wait_ge(tab_in, 16)
                    bank = p_wide[1 - n]
                    src = bank[:].rearrange("p (h s d) -> p h s d", h=H, s=2)
                    table = tab[:, t.window].rearrange("p c (s d) -> p c s d", s=2)
                    dve.tensor_tensor(rope_a[:, n], bank[:].rearrange("p (h d) -> p h d", h=H),
                                      tab[:, t.window, 2 * n].unsqueeze(1).to_broadcast([P, H, D]), ALU.mult)
                    dst = rope_b[:, n].rearrange("p h (s d) -> p h s d", s=2)
                    for s in range(2):
                        ins = dve.tensor_tensor(dst[:, :, s], src[:, :, 1 - s],
                                                table[:, 2 * n + 1, s].unsqueeze(1).to_broadcast([P, H, D // 2]),
                                                ALU.mult)
                    ins.then_inc(raised, 1)

                def squared_norms(n):
                    need(dve, pool_r[n], t.done(1))
                    dve.tensor_reduce(ss[:, n * H:(n + 1) * H], sq[:, n * H:(n + 1) * H], AX.X, ALU.add)\
                        .then_inc(dve_ss[n], 1)
                    dve.wait_ge(dve_ss[n], t.done(1, 1))
                    dve.tensor_scalar(rt[:, n * H:(n + 1) * H], ss[:, n * H:(n + 1) * H], NORM_FLOOR, None, ALU.max)\
                        .then_inc(dve_rt[n], 1)

                def values(group):
                    if group == 0:
                        dve.wait_ge(act_exp, a.done(H, H))
                        dve.reciprocal(rinv[:], rsum[:]).then_inc(dve_rinv, 1)
                        dve.wait_ge(dve_rinv, a.done(1, 1))
                        need(dve, pe_oT, a.done(1))
                    dve.wait_ge(pe_pv, a.done(2, group + 1))
                    dve.tensor_tensor(o[:, group * 256:(group + 1) * 256].rearrange("p (h d) -> p h d", h=4),
                                      p_val[:, 0:256].rearrange("p (h d) -> p h d", h=4),
                                      rinv[:, 4 * group:4 * group + 4].unsqueeze(2).to_broadcast([P, 4, D]),
                                      ALU.mult).then_inc(dve_o, 1)

                if a:
                    least_of(0)
                if g:
                    n = g.slot(2)
                    dve.wait_ge(pool_rstd, g.done(1, 1))
                    need(dve, pe_hT, g.uses(2))
                    dve.tensor_scalar(hn[:, n, 0:P], mid[:, n, 0:P], mv[:, n, 0:1], rstd[:, n:n + 1],
                                      ALU.subtract, ALU.mult)
                    dve.tensor_scalar(hn[:, n, P:E], shifted[:, n], mv[:, n, 0:1], rstd[:, n:n + 1],
                                      ALU.subtract, ALU.mult).then_inc(dve_hn, 1)
                if e and e.layer == 1:
                    n = e.slot(2)
                    dve.wait_ge(pool_frstd, e.done(1, 1 - LAYER))
                    need(dve, out_out[n], 16 * e.uses(2, -LAYER // 2))
                    dve.tensor_scalar(fo[:, n], xf[:, n], fmv[:, n, 0:1], frstd[:, n:n + 1],
                                      ALU.subtract, ALU.mult).then_inc(dve_out, 1)
                if a:
                    least_of(1)
                if c:
                    n = c.slot(2)
                    dve.wait_ge(pe_wo, c.done(1, 1))
                    need(dve, mid_out[n], 16 * c.uses(2))
                    need(dve, pool_res, c.done(1, -1))
                    dve.tensor_tensor(mid[:, n], p_mix[:, 0:E], x_sb[:, c.slot(4), 0:E], ALU.add).then_inc(dve_mid, 1)
                if t:
                    rotary(1, dve_kr, pool_k)
                    squared_norms(1)
                if st_.even and f:
                    dve.wait_ge(pe_hT, pair_done(f, 1, 1))
                    for k in range(KE):
                        ins = dve.tensor_scalar(hv[:, k], p_mix[:, k * 2 * P:(k + 1) * 2 * P],
                                                par_s[:, f.layer, k:k + 1], par_s[:, f.layer, KE + k:KE + k + 1],
                                                ALU.mult, ALU.add)
                    ins.then_inc(dve_hv, 1)
                if a and st_.even and f:
                    values(0)
                if t:
                    rotary(0, dve_qr, dve_q)
                if a and not (st_.even and f):
                    values(0)
                if t and not (st_.even and f):
                    squared_norms(0)
                if st_.even and f:
                    dve.wait_ge(act_hT, pair_done(f, 1, 1))
                    dve.tensor_tensor(hT_l[:], hv[:], hT_h[:].bitcast(F32), ALU.subtract).then_inc(dve_hT, 1)
                    if t:
                        squared_norms(0)
                elif u:
                    turned_x(u)
                if t:
                    dve.wait_ge(dve_qr, t.done(1, 1))
                    need(dve, pe_qT, t.done(1))
                    dve.tensor_tensor(qn[:].rearrange("p (h d) -> p h d", h=H), rope_a[:, 0], rope_b[:, 0], ALU.add)\
                        .then_inc(dve_q, 1)
                if a:
                    values(1)
                if st_.even and f:

                    def gated(n):
                        rows = P if n < HF else HR
                        col = 2 * KE + (n if n < HF else 2 * HF)
                        dve.wait_ge(act_gelu, pair_done(f, HF + 1, n + 1))
                        need(dve, act_gT, pair_done(f, HF + 1, n - 2))
                        need(dve, dve_gT, pair_done(f, HF + 1, n - 2))
                        dve.scalar_tensor_tensor(gt[0:rows, n % 3], p_wide[(n + 1) % 2][0:rows, 0:2 * P],
                                                 par_s[0:rows, f.layer, col:col + 1], gel[0:rows, n % 2],
                                                 ALU.add, ALU.mult).then_inc(dve_gt, 1)

                    def low(n):
                        rows = P if n < HF else HR
                        dve.wait_ge(act_gT, pair_done(f, HF + 1, n + 1))
                        dve.tensor_tensor(gT_l[0:rows, n], gt[0:rows, n % 3], gT_h[0:rows, n].bitcast(F32),
                                          ALU.subtract).then_inc(dve_gT, 1)

                    gated(0)
                    for n in range(1, HF + 1):
                        gated(n)
                        low(n - 1)
                        if u and n == 1:
                            turned_x(u)
                    low(HF)

            all_steps(dve, step, peel_last=True)

        @block.tensor
        def _(pe):
            def step(st_):
                a, t, c, e = (st_.tile(n) for n in (1, 0, 2, 5))
                f = st_.tile(4) if st_.even else None
                u = st_.tile(-1)
                last_mid, last_pair = st_.tile(3), st_.tile(5)

                def mixed_bank_free():
                    if last_mid:
                        pe.wait_ge(dve_mid, last_mid.done(1, 1))
                    elif st_.tile(6):
                        pe.wait_ge(dve_x, st_.tile(6).done(1, 1))
                    if not st_.even and last_pair:
                        pe.wait_ge(dve_hv, pair_done(last_pair, 1, 1))

                def arrived(name, tile):
                    if name == "qkv":
                        if tile.is_number(LAYER):
                            pe.wait_ge(w_in[name], 32)
                    elif tile.is_number(0) or tile.is_number(LAYER):
                        pe.wait_ge(w_in[name], 32 * (tile.layer + 1))

                def turn_qk():
                    need(pe, act_pT, a.done(4))
                    for n, (src, ready, raised) in enumerate(((qn, dve_q, pe_qT), (kn, pool_k, pe_kT))):
                        pe.wait_ge(ready, a.done(1, 1))
                        for m in range(H // 2):
                            ins = pe.transpose(p_turn[n][:, m * P:(m + 1) * P], src[:, m * P:(m + 1) * P], ident[:])
                        ins.then_inc(raised, 1)

                def scores(group):
                    if group == 0:
                        pe.wait_ge(dve_qT, a.done(1, 1))
                        pe.wait_ge(dve_kT, a.done(1, 1))
                        need(pe, dve_least, a.done(H))
                    else:
                        pe.wait_ge(dve_least, a.done(H, 4))
                    cols = key_columns(a)
                    for h in range(4 * group, 4 * group + 4):
                        rows, m, c0 = slice(h % 2 * D, (h % 2 + 1) * D), h // 2, h % 4 // 2 * 2 * P
                        kh, kl = (x_[rows, m].rearrange("p b t -> p (b t)")[:, cols] for x_ in (kT_h, kT_l))
                        ins = three_pass(pe, p_score[h % 2][:, c0 + cols.start:c0 + cols.stop],
                                         (qT_h[rows, m], qT_l[rows, m]), (kh, kl), True, True)
                    ins.then_inc(pe_s, 1)

                def turn_probs(group):
                    for n in range(2):
                        pe.wait_ge(act_exp, a.done(H, 4 * group + 2 * n + 2))
                        if group == 1:
                            pe.wait_ge(act_pT, a.done(4, n + 1))
                        for hh in range(2):
                            h = 4 * group + 2 * n + hh
                            for b in blocks_of(a):
                                ins = pe.transpose(p_turn[n][:, (2 * hh + b) * P:(2 * hh + b + 1) * P],
                                                   prob[:, h, b * P:(b + 1) * P], ident[:])
                        ins.then_inc(pe_pT, 1)

                def values(group):
                    if group == 0:
                        pe.wait_ge(act_v, a.done(1, 1))
                        if c:
                            pe.wait_ge(dve_oT, c.done(1, 1))
                    else:
                        pe.wait_ge(dve_o, a.done(2, 1))
                    pe.wait_ge(act_pT, a.done(4, 2 * group + 2))
                    blocks = blocks_of(a)
                    for hh in range(4):
                        h = 4 * group + hh
                        for b in blocks:
                            slot = a.slot(4) if b == a.slot(2) else (a.off - 1) % 4
                            ins = pe.matmul(p_val[:, hh * D:(hh + 1) * D], pT[:, group, hh, b],
                                            v[:, slot, h * D:(h + 1) * D], start=b == blocks[0], stop=b == blocks[-1])
                    ins.then_inc(pe_pv, 1)

                def project(n, bank, raised, chunks=range(KE)):
                    for k in chunks:
                        cols = slice(n * INNER, (n + 1) * INNER)
                        ins = three_pass(pe, bank[:], (xT_h[:, k], xT_l[:, k]), (wqkv[0][:, k, cols], wqkv[1][:, k, cols]),
                                         k == 0, k == KE - 1)
                    if k == KE - 1:
                        ins.then_inc(raised, 1)

                def turn_x(u):
                    n = u.slot(4)
                    pe.wait_ge(x_in[n], 32 * u.uses(4, 1))
                    for k in range(KE):
                        ins = pe.transpose(p_mix[:, k * P:(k + 1) * P], x_sb[:, n, k * E:k * E + P], ident[:])
                    ins.then_inc(pe_xT, 1)

                if t and t.is_number(0):
                    turn_x(t)
                if a:
                    turn_qk()
                if c:
                    pe.wait_ge(dve_o, c.done(2, 2))
                    for m in range(INNER // P):
                        ins = pe.transpose(p_val[:, m * P:(m + 1) * P], o[:, m * P:(m + 1) * P], ident[:])
                    ins.then_inc(pe_oT, 1)
                if e:
                    if t:
                        pe.wait_ge(dve_xT, t.done(1, 1))
                    else:
                        mixed_bank_free()
                    arrived("w2", e)
                    pair = Tile(e.i, e.off - e.slot(2), e.layer)
                    pe.wait_ge(dve_gT, pair_done(pair, HF + 1, HF - 1))
                    c0 = e.slot(2) * P
                    for n in range(HF + 1):
                        rows = P if n < HF else HR
                        if n >= HF - 1:
                            pe.wait_ge(dve_gT, pair_done(pair, HF + 1, n + 1))
                        ins = three_pass(pe, p_mix[:, 0:E], (gT_h[0:rows, n, c0:c0 + P], gT_l[0:rows, n, c0:c0 + P]),
                                         (w2[0][0:rows, n], w2[1][0:rows, n]), n == 0, n == HF)
                    ins.then_inc(pe_w2, 1)
                if t:
                    if not e:
                        pe.wait_ge(dve_xT, t.done(1, 1))
                    need(pe, act_v, t.done(1))
                    if not st_.even and last_pair:
                        pe.wait_ge(dve_gt, pair_done(last_pair, HF + 1, HF + 1))
                    arrived("qkv", t)
                    project(1, p_wide[0], pe_k, [0])
                if a:
                    scores(0)
                if t:
                    project(1, p_wide[0], pe_k, [1])
                if c:
                    if e:
                        pe.wait_ge(dve_x, e.done(1, 1))
                    pe.wait_ge(dve_oT, c.done(1, 1))
                    arrived("wo", c)
                    for m in range(INNER // P):
                        ins = three_pass(pe, p_mix[:, 0:E], (oT_h[:, m], oT_l[:, m]), (wo[0][:, m], wo[1][:, m]),
                                         m == 0, m == INNER // P - 1)
                    ins.then_inc(pe_wo, 1)
                if a:
                    scores(1)
                    turn_probs(0)
                if t:
                    need(pe, dve_qr, t.done(1))
                    project(0, p_wide[1], pe_q)
                if f:
                    if c:
                        pe.wait_ge(dve_mid, c.done(1, 1))
                    elif e:
                        pe.wait_ge(dve_x, e.done(1, 1))
                    pe.wait_ge(dve_hn, f.done(1, 2))
                    for k in range(KE):
                        for m in range(2):
                            ins = pe.transpose(p_mix[:, (2 * k + m) * P:(2 * k + m + 1) * P],
                                               hn[:, m, k * P:(k + 1) * P], ident[:])
                    ins.then_inc(pe_hT, 1)
                if a:
                    values(0)
                    turn_probs(1)
                if t:
                    pe.wait_ge(dve_kr, t.done(1, 1))
                    project(2, p_wide[0], pe_v)
                if u and not f:
                    if c:
                        pe.wait_ge(dve_mid, c.done(1, 1))
                    elif t:
                        pe.wait_ge(dve_xT, t.done(1, 1))
                    turn_x(u)
                if a:
                    values(1)
                if f:
                    pe.wait_ge(dve_hT, pair_done(f, 1, 1))
                    arrived("w1", f)
                    for n in range(HF + 1):
                        if n == 0 and t:
                            pe.wait_ge(dve_qr, t.done(1, 1))
                        elif n == 1 and t:
                            pe.wait_ge(act_v, t.done(1, 1))
                        elif n >= 2:
                            pe.wait_ge(dve_gt, pair_done(f, HF + 1, n - 1))
                        bank = p_wide[(n + 1) % 2]
                        parts = [(n, 0, P), (HF + n, 2 * P, P)] if n < HF else [(2 * HF, 0, GR + HR)]
                        for chunk, at, width in parts:
                            for k in range(KE):
                                cols = slice(chunk * P, chunk * P + width)
                                ins = three_pass(pe, bank[0:width, at:at + 2 * P],
                                                 (w1[0][:, k, cols], w1[1][:, k, cols]), (hT_h[:, k], hT_l[:, k]),
                                                 k == 0, k == KE - 1)
                        ins.then_inc(pe_w1, 1)
                        if u and n == 1:
                            pe.wait_ge(dve_hv, pair_done(f, 1, 1))
                            turn_x(u)

            all_steps(pe, step, peel_last=True)


def kernel(**inputs):
    import numpy as np
    import concourse.bacc as bacc
    from concourse.bass_utils import run_bass_kernel_spmd

    a = {n.removeprefix("L0_"): np.asarray(v) for n, v in inputs.items()}

    def chunks(w, width=None):
        rows = -(-w.shape[0] // P) * P
        full = np.zeros((rows, w.shape[1]), w.dtype)
        full[:w.shape[0]] = w
        return full.reshape(rows // P, P, w.shape[1]).transpose(1, 0, 2)

    def by_chunk(w):
        tail = np.zeros(w.shape[:-1] + (P,), w.dtype)
        tail[..., 0:HR] = w[..., HF * P:HID]
        tail[..., GR:GR + HR] = w[..., HID + HF * P:]
        return np.concatenate([w[..., 0:HF * P], w[..., HID:HID + HF * P], tail], axis=-1)

    w_all = np.concatenate([
        np.concatenate([chunks(w).reshape(P, -1) for w in (
            a["ffn_wqkv"][n], a["ffn_wo"][n], by_chunk(a["ffn_w1"][n]), a["ffn_w2"][n])], axis=1)
        for n in range(DEPTH)], axis=1)
    par = np.stack([np.concatenate([
        a["ffn_ln_g"][n].reshape(KE, P).T, a["ffn_ln_b"][n].reshape(KE, P).T,
        by_chunk(a["ffn_b1"][n]).reshape(W1C, P).T], axis=1) for n in range(DEPTH)], axis=1)
    swap = lambda s: np.concatenate([s[..., D // 2:], s[..., :D // 2]], axis=-1)
    qs, ks = a["ffn_q_scale"], a["ffn_k_scale"]
    tab_scale = np.concatenate([qs, swap(qs), ks, swap(ks)], axis=-1)

    f = np.float32
    half_idx = np.arange(0, D, 2, dtype=f)
    inv_freq = (f(1) / np.power(f(10000), half_idx / f(D))).astype(f)
    pos = np.arange(S, dtype=f)
    angle = np.tile((pos[:, None] * inv_freq[None, :]).astype(f), (1, 2)).astype(np.float64)
    base = ((half_idx + f(0.4 * D)) / f(1.4 * D)).astype(f).astype(np.float64)
    power = ((pos - S // 2) / f(P // 2)).astype(np.float64)
    decay = np.tile(base[None, :] ** power[:, None], (1, 2))
    sign = np.where(np.arange(D) < D // 2, -1.0, 1.0)
    tab_base = np.concatenate([-8 * np.cos(angle) * decay, -8 * sign * np.sin(angle) * decay,
                               np.cos(angle) / decay, sign * np.sin(angle) / decay], axis=1)
    tab_base = tab_base.astype(f).reshape(NW, P, 4 * D).transpose(1, 0, 2)
    i, j = np.arange(P)[:, None], np.arange(P)[None, :]
    own, prev = np.where(j > i, f(MASK2), f(0)), np.where(j < i, f(MASK2), f(0))
    masks = np.stack([np.concatenate([own, prev], 1), np.concatenate([prev, own], 1)], axis=1)
    cmask = np.zeros((P, S), f)
    cmask[:, S - P:] = np.where(j > i, f(MASK1), f(0))

    arrays = {
        "x": a["attn_x"].reshape(B * S, E),
        "wqk": chunks(np.concatenate([a["attn_wq"], a["attn_wk"]], axis=1)),
        "wv": chunks(a["attn_wv"]),
        "wo0": a["attn_wo"],
        "bqk": np.concatenate([a["attn_bq"], a["attn_bk"]])[:, None],
        "bvo": np.concatenate([a["attn_bv"], a["attn_bo"]]),
        "w_all": w_all,
        "b2": a["ffn_b2"],
        "par": par,
        "tab_base": tab_base,
        "tab_scale": tab_scale,
        "masks": masks,
        "cmask": cmask,
        "eye": np.eye(P, dtype=f),
        "zrow": np.zeros((DEPTH * B, E), f),
    }
    nc = bacc.Bacc("TRN2", target_bir_lowering=False, num_devices=1)
    arrays = {f"in_{n}": np.ascontiguousarray(v) for n, v in arrays.items()}
    t = {n[3:]: nc.dram_tensor(n, v.shape, F32, kind="ExternalInput").ap() for n, v in arrays.items()}
    out = nc.dram_tensor("out_rows", (B * S, E), F32, kind="ExternalOutput").ap()
    post_norm_block(nc, out=out, **t)
    got = run_bass_kernel_spmd(nc, [arrays], core_ids=[0])
    return got.results[0]["out_rows"].reshape(B, S, E)
```
